# Optimizing a Trainium2 kernel written in Bass

```python
import numpy as np
import jax
import jax.numpy as jnp

def _softmax(x, axis=-1):
    return jax.nn.softmax(x, axis=axis)

def _gelu(x):
    return jax.nn.gelu(x, approximate=True)

def _silu(x):
    return jax.nn.silu(x)

def _sigmoid(x):
    return jax.nn.sigmoid(x)

def _layernorm(x, axis=-1, eps=1e-05):
    m = jnp.mean(x, axis=axis, keepdims=True)
    v = jnp.var(x, axis=axis, keepdims=True)
    return (x - m) / jnp.sqrt(v + eps)

def _scatter_add(tgt, idx, src, axis=0):
    return tgt.at[idx].add(src)

def _segment_sum(src, seg, n):
    return jax.ops.segment_sum(src, seg, n)
kernel_name = 'mk_gnn_preln_d1_gnn_r32_f0fe2a'

def setup_inputs(seed: int=0):
    np.random.seed(seed)
    _w = jnp.asarray

    def _rec_inputs():
        import jax
        import jax.numpy as jnp
        _gk = jax.random.key(seed)
        x = -1.686e-05 + 1 * jax.random.normal(jax.random.fold_in(_gk, 1), (50000, 160), jnp.float32)
        src = jax.random.randint(jax.random.fold_in(_gk, 2), (25000,), 0, 50000, jnp.int32)
        dst = jnp.minimum((50000 * jax.random.uniform(jax.random.fold_in(_gk, 3), (25000,)) ** 2.0).astype(jnp.int32), 49999)
        _o = jnp.argsort(dst, stable=True)
        src = src[_o]
        dst = dst[_o]
        edge_attr_32 = 0.000196303 + 1.00016 * jax.random.normal(jax.random.fold_in(_gk, 11), (25000, 32), jnp.float32)
        node_vec1 = -0.00915711 + 0.999674 * jax.random.normal(jax.random.fold_in(_gk, 13), (50000, 1), jnp.float32)
        return (x, src, dst, edge_attr_32, node_vec1)
    x, src, dst, edge_attr_32, node_vec1 = _rec_inputs()

    def _L0_gnn_setup():
        import jax, jax.numpy as jnp
        import numpy as np
        MUL0_N, MUL1_N = (64, 32)
        MUL0_E, MUL1_E = (8, 8)
        MUL0_H, MUL1_H = (64, 32)
        N_NODES, N_EDGES = (50000, 25000)
        D_NODE = MUL0_N + 3 * MUL1_N
        D_EDGE = MUL0_E + 3 * MUL1_E
        D_HID = MUL0_H + 3 * MUL1_H

        def _split(x, mul0, mul1):
            s = x[..., :mul0]
            v = x[..., mul0:].reshape(x.shape[0], mul1, 3)
            return (s, v)

        def fctp_messages(x, e, W1, W2, W3, W4):
            xs, xv = _split(x, MUL0_N, MUL1_N)
            es, ev = _split(e, MUL0_E, MUL1_E)
            inv_sqrt2 = 1.0 / np.sqrt(2.0)
            s1 = jnp.einsum('ea,eb,abc->ec', xs, es, W1) * (1.0 / np.sqrt(MUL0_N * MUL0_E))
            s2 = jnp.einsum('eai,ebi,abc->ec', xv, ev, W2) * (1.0 / (np.sqrt(3.0) * np.sqrt(MUL1_N * MUL1_E)))
            out_s = (s1 + s2) * inv_sqrt2
            v1 = jnp.einsum('ea,ebi,abc->eci', xs, ev, W3) * (1.0 / np.sqrt(MUL0_N * MUL1_E))
            v2 = jnp.einsum('eai,eb,abc->eci', xv, es, W4) * (1.0 / np.sqrt(MUL1_N * MUL0_E))
            out_v = (v1 + v2) * inv_sqrt2
            return jnp.concatenate([out_s, out_v.reshape(out_v.shape[0], -1)], axis=-1)
        key = jax.random.key(seed)
        ks = jax.random.split(key, 12)
        node_features = jax.random.normal(ks[0], (N_NODES, D_NODE), dtype=jnp.float32)
        edge_index = jax.random.randint(ks[1], (2, N_EDGES), 0, N_NODES, dtype=jnp.int64)
        edge_attr_tensor = jax.random.normal(ks[2], (N_EDGES, D_EDGE), dtype=jnp.float32)
        node_attr_scalar_raw = jax.random.normal(ks[3], (N_NODES, 1), dtype=jnp.float32)
        W1 = jax.random.normal(ks[4], (MUL0_N, MUL0_E, MUL0_H), dtype=jnp.float32)
        W2 = jax.random.normal(ks[5], (MUL1_N, MUL1_E, MUL0_H), dtype=jnp.float32)
        W3 = jax.random.normal(ks[6], (MUL0_N, MUL1_E, MUL1_H), dtype=jnp.float32)
        W4 = jax.random.normal(ks[7], (MUL1_N, MUL0_E, MUL1_H), dtype=jnp.float32)
        Wm = jax.random.normal(ks[8], (D_HID, D_HID), dtype=jnp.float32) / np.sqrt(D_HID)
        bm = jnp.zeros((D_HID,), dtype=jnp.float32)
        Wu = jax.random.normal(ks[9], (D_NODE + D_HID, D_NODE), dtype=jnp.float32) / np.sqrt(D_NODE + D_HID)
        bu = jnp.zeros((D_NODE,), dtype=jnp.float32)
        return {'node_features': node_features, 'edge_index': edge_index, 'edge_attr_tensor': edge_attr_tensor, 'node_attr_scalar_raw': node_attr_scalar_raw, 'W1': W1, 'W2': W2, 'W3': W3, 'W4': W4, 'Wm': Wm, 'bm': bm, 'Wu': Wu, 'bu': bu}
    _L0_gnn_all = _L0_gnn_setup()
    _L0_gnn_in = {k: v for k, v in _L0_gnn_all.items() if k in ('W1', 'W2', 'W3', 'W4', 'Wm', 'bm', 'Wu', 'bu')}
    del _L0_gnn_all
    return {'x': x, 'src': src, 'dst': dst, 'edge_attr_32': edge_attr_32, 'node_vec1': node_vec1, 'L0_gnn_W1': _L0_gnn_in['W1'], 'L0_gnn_W2': _L0_gnn_in['W2'], 'L0_gnn_W3': _L0_gnn_in['W3'], 'L0_gnn_W4': _L0_gnn_in['W4'], 'L0_gnn_Wm': _L0_gnn_in['Wm'], 'L0_gnn_bm': _L0_gnn_in['bm'], 'L0_gnn_Wu': _L0_gnn_in['Wu'], 'L0_gnn_bu': _L0_gnn_in['bu']}

def reference(x, src, dst, edge_attr_32, node_vec1, L0_gnn_W1, L0_gnn_W2, L0_gnn_W3, L0_gnn_W4, L0_gnn_Wm, L0_gnn_bm, L0_gnn_Wu, L0_gnn_bu):
    import jax
    import jax.numpy as jnp

    def _L0_gnn_ref(node_features, edge_index, edge_attr_tensor, node_attr_scalar_raw, W1, W2, W3, W4, Wm, bm, Wu, bu):
        import jax, jax.numpy as jnp
        import numpy as np
        MUL0_N, MUL1_N = (64, 32)
        MUL0_E, MUL1_E = (8, 8)
        MUL0_H, MUL1_H = (64, 32)
        N_NODES, N_EDGES = (50000, 25000)
        D_NODE = MUL0_N + 3 * MUL1_N
        D_EDGE = MUL0_E + 3 * MUL1_E
        D_HID = MUL0_H + 3 * MUL1_H

        def _split(x, mul0, mul1):
            s = x[..., :mul0]
            v = x[..., mul0:].reshape(x.shape[0], mul1, 3)
            return (s, v)

        def fctp_messages(x, e, W1, W2, W3, W4):
            xs, xv = _split(x, MUL0_N, MUL1_N)
            es, ev = _split(e, MUL0_E, MUL1_E)
            inv_sqrt2 = 1.0 / np.sqrt(2.0)
            s1 = jnp.einsum('ea,eb,abc->ec', xs, es, W1) * (1.0 / np.sqrt(MUL0_N * MUL0_E))
            s2 = jnp.einsum('eai,ebi,abc->ec', xv, ev, W2) * (1.0 / (np.sqrt(3.0) * np.sqrt(MUL1_N * MUL1_E)))
            out_s = (s1 + s2) * inv_sqrt2
            v1 = jnp.einsum('ea,ebi,abc->eci', xs, ev, W3) * (1.0 / np.sqrt(MUL0_N * MUL1_E))
            v2 = jnp.einsum('eai,eb,abc->eci', xv, es, W4) * (1.0 / np.sqrt(MUL1_N * MUL0_E))
            out_v = (v1 + v2) * inv_sqrt2
            return jnp.concatenate([out_s, out_v.reshape(out_v.shape[0], -1)], axis=-1)
        row, col = (edge_index[0], edge_index[1])
        tp = fctp_messages(node_features[col], edge_attr_tensor, W1, W2, W3, W4)
        messages = tp @ Wm + bm
        agg = jax.ops.segment_sum(messages, row, num_segments=N_NODES)
        upd = jnp.concatenate([node_features, agg], axis=-1) @ Wu + bu
        return node_features + upd
    edge_index = jnp.stack([src, dst])
    h = jnp.maximum(_layernorm(x, axis=-1), 0.0)
    x = x + _L0_gnn_ref(h, edge_index, edge_attr_32, node_vec1, L0_gnn_W1, L0_gnn_W2, L0_gnn_W3, L0_gnn_W4, L0_gnn_Wm, L0_gnn_bm, L0_gnn_Wu, L0_gnn_bu)
    return x

_drawn_inputs = setup_inputs


def setup_inputs(seed=0):
    import zlib

    import numpy as np

    out = dict(_drawn_inputs(seed))
    spreads = {'L0_gnn_bm': (0.0, 0.1), 'L0_gnn_bu': (0.0, 0.1)}
    factors = {}
    for name, (base, spread) in spreads.items():
        noise = np.random.default_rng([zlib.crc32(name.encode()), seed]).standard_normal(out[name].shape)
        drawn = base * np.exp(spread * noise) if base else spread * noise
        out[name] = jnp.asarray(drawn.astype(out[name].dtype))
    for name, factor in factors.items():
        out[name] = (out[name] * factor).astype(out[name].dtype)
    return out
```

```python
import numpy as np
import concourse.bass as bass
from concourse import mybir
from contextlib import ExitStack

N_NODES, N_EDGES = 50000, 25000
D, DE = 160, 32
MUL0, MUL1, MB = 64, 32, 8
P = 128
EPS = 1e-5

RPP = 8
GROUP = P * RPP
NG = -(-N_NODES // GROUP)
TAIL_ROWS = N_NODES - (NG - 1) * GROUP
TAIL_P = TAIL_ROWS // RPP
TAIL_A = TAIL_P // 16 * 16
XS = 4

TPC = 4
CHUNK = TPC * P
NC = -(-N_EDGES // CHUNK)
E_PAD = NC * CHUNK
OUT_ROWS = N_NODES + P

C_S1 = 1.0 / np.sqrt(2.0) / np.sqrt(MUL0 * MB)
C_S2 = 1.0 / np.sqrt(2.0) / (np.sqrt(3.0) * np.sqrt(MUL1 * MB))
C_V1 = 1.0 / np.sqrt(2.0) / np.sqrt(MUL0 * MB)
C_V2 = 1.0 / np.sqrt(2.0) / np.sqrt(MUL1 * MB)


def gnn_program(nc, x, dst_cols, src_cols, src_rows, attr_t, w1, w2, w3, w4, wm_t, bm, wu_top,
                wu_bot, bu, eye, eye160, delta, earlier, spare, out):
    f32, i32 = mybir.dt.float32, mybir.dt.int32
    ALU, ACT = mybir.AluOpType, mybir.ActivationFunctionType
    ctx = ExitStack()

    def sb(name, shape, dt=f32):
        return ctx.enter_context(nc.sbuf_tensor(name, shape, dt))

    def sem(name):
        return ctx.enter_context(nc.semaphore(name))

    with ctx:
        bank = [ctx.enter_context(nc.psum_tensor(f"bank{i}", [P, 512], f32)) for i in range(8)]

        ident = sb("ident", [P, P])
        deltas = sb("deltas", [P, MUL1])
        before = sb("before", [P, P])
        spare_row = sb("spare_row", [P, 1])
        w1_raw, w1_sb = sb("w1_raw", [P, 4, MUL0]), sb("w1_sb", [P, 4, MUL0])
        w2_raw, w2_sb = sb("w2_raw", [P, 2, MUL0]), sb("w2_sb", [P, 2, MUL0])
        w3_raw, w3_sb = sb("w3_raw", [MUL0, 2, P]), sb("w3_sb", [MUL0, 2, P])
        w4_raw, w4_sb = sb("w4_raw", [P, 2, MUL1]), sb("w4_sb", [P, 2, MUL1])
        wmT_a, wmT_b = sb("wmT_a", [P, D + 1]), sb("wmT_b", [D - P, D + 1])
        wub_a, wub_b = sb("wub_a", [P, D]), sb("wub_b", [D - P, D])
        wc_a, wc_b = sb("wc_a", [P, D]), sb("wc_b", [D - P + 1, D])
        wut_raw_a, wut_a = sb("wut_raw_a", [P, 2, D]), sb("wut_a", [P, 2, D])
        wut_raw_b, wut_b = sb("wut_raw_b", [P, D]), sb("wut_b", [P, D])
        eps_ap = sb("eps_ap", [P, 1])
        eye_a, eye_b = sb("eye_a", [P, 2, D]), sb("eye_b", [P, D])

        x_sb = sb("x_sb", [P, XS, RPP, D])
        y_sb = sb("y_sb", [P, 2, RPP, D])
        hn = sb("hn", [P, 2, RPP // 2, 384])
        hT_a, hT_b = sb("hT_a", [P, 2, 512]), sb("hT_b", [P, 2, 256])
        bst = sb("bst", [P, RPP, 6])
        mv = sb("mv", [P, RPP, 2])
        std = sb("std", [P, RPP])
        r0, r1, r2 = sb("r0", [P, RPP]), sb("r1", [P, RPP]), sb("r2", [P, RPP])
        rstd = sb("rstd", [P, 2, RPP])
        nbias = sb("nbias", [P, 2, RPP])

        dst_sb = sb("dst_sb", [P, 2, TPC], i32)
        src_sb = sb("src_sb", [P, 2, TPC], i32)
        src_f = sb("src_f", [P, TPC])
        src_row = sb("src_row", [P, 2, CHUNK], i32)
        attr = sb("attr", [P, 2, 8, CHUNK])
        xg = sb("xg", [P, 2, TPC, D])
        hg = sb("hg", [P, 2, TPC, 5, 4, 32])
        xsT = sb("xsT", [MUL0, CHUNK])
        p_xs = sb("p_xs", [P, 2, 2, CHUNK])
        p_v2 = sb("p_v2", [P, 3, 2, CHUNK])
        p_d = sb("p_d", [P, 3, 2, CHUNK])
        p_y = sb("p_y", [P, 2, 3, CHUNK])
        d_part = sb("d_part", [P, 2, CHUNK])
        d_sum = sb("d_sum", [P, 2, CHUNK])
        v_sum = sb("v_sum", [P, 3, CHUNK])
        equal = sb("equal", [P, TPC, P])
        scrap = sb("scrap", [P, TPC, P])
        n_before = sb("n_before", [P, TPC])
        to_spare = sb("to_spare", [P, TPC])
        shift = sb("shift", [P, TPC])
        row_f = sb("row_f", [P, 2, TPC])
        row_i = sb("row_i", [P, 2, TPC], i32)
        tp_sb = sb("tp_sb", [P, TPC, D + 1])
        tT_a, tT_b = sb("tT_a", [P, 2, 256]), sb("tT_b", [D - P + 1, 2, 256])
        msg = sb("msg", [P, 2, TPC, D])
        zero_rows = sb("zero_rows", [P, D])

        w_in = sem("w_in")
        w_ready = sem("w_ready")
        wc_mm = sem("wc_mm")
        x_in = [sem(f"x_in{s}") for s in range(XS)]
        y_out = [sem(f"y_out{s}") for s in range(2)]
        stats_done, mv_ready, std_ready = sem("stats_done"), sem("mv_ready"), sem("std_ready")
        rstd_step, norm_ready = sem("rstd_step"), sem("norm_ready")
        h_ready, hT_full, hT_ready, out_full, y_ready = (
            sem(n) for n in ("h_ready", "hT_full", "hT_ready", "out_full", "y_ready"))
        prep = sem("prep")
        dst_in = [sem(f"dst_in{s}") for s in range(2)]
        src_in = [sem(f"src_in{s}") for s in range(2)]
        attr_in = [sem(f"attr_in{s}") for s in range(2)]
        xg_in = [sem(f"xg_in{s}") for s in range(2)]
        g_stats, g_mv, g_std, g_step, g_norm, g_h = (
            sem(n) for n in ("g_stats", "g_mv", "g_std", "g_step", "g_norm", "g_h"))
        front_full, back_full, tp_full = sem("front_full"), sem("back_full"), sem("tp_full")
        taken = sem("taken")
        xsT_ready, tp_ready, tT_ready, msg_ready = (
            sem(n) for n in ("xsT_ready", "tp_ready", "tT_ready", "msg_ready"))
        d_part_ready, d_ready, v_ready = sem("d_part_ready"), sem("d_ready"), sem("v_ready")
        d_used, v_used = sem("d_used"), sem("v_used")
        eq_ready, eq_step, row_ready = sem("eq_ready"), sem("eq_step"), sem("row_ready")
        spare_in = sem("spare_in")
        added = sem("added")
        msg_free = sem("msg_free")
        passed_dve, passed_pool = sem("passed_dve"), sem("passed_pool")

        N_W = 24
        block = ctx.enter_context(nc.Block())

        def bcast(ap, shape):
            return ap.broadcast_to(shape)

        def hg_block(s, t, n):
            return hg[:, s, t, n].rearrange("p b a -> p (b a)")

        def hg_scalars(s, t):
            return hg[:, s, t].rearrange("p n b a -> p (n b a)")[:, 96:96 + P]

        def rows_of(dram, g):
            return dram[bass.ds(g * GROUP, GROUP), :].rearrange("(p r) d -> p r d", r=RPP)

        TB = (NG - 1) * GROUP

        def tail_of(dram, p0, p1):
            return dram[TB + p0 * RPP:TB + p1 * RPP, :].rearrange("(p r) d -> p r d", r=RPP)

        @block.sync
        def _(sp):
            loads = [
                (ident[:], eye), (deltas[:], delta), (before[:], earlier), (spare_row[:], spare),
                (w1_raw[:], w1), (w2_raw[:], w2), (w3_raw[:], w3), (w4_raw[:], w4),
                (wmT_a[:, 0:D], wm_t[0:P, :]), (wmT_b[:, 0:D], wm_t[P:D, :]),
                (wmT_a[:, D:D + 1], bm[0:P, :]), (wmT_b[:, D:D + 1], bm[P:D, :]),
                (wub_a[:], wu_bot[0:P, :]), (wub_b[:], wu_bot[P:D, :]),
                (wut_raw_a[:, 0], wu_top[0:P, :]), (wut_raw_a[:, 1], wu_top[D - P:D, :]),
                (eye_a[:, 0], eye160[0:P, :]), (eye_a[:, 1], eye160[D - P:D, :]),
                (wut_raw_b[0:32, :], wu_top[P:D, :]), (wut_raw_b[32:33, :], bu),
                (wut_raw_b[64:65, :], bu), (wut_raw_b[96:P, :], wu_top[0:32, :]),
                (eye_b[0:32, :], eye160[P:D, :]), (eye_b[96:P, :], eye160[0:32, :]),
            ]
            assert len(loads) == N_W
            sp.wait_ge(prep, 1)
            sp.dma_start(x_sb[:, 0], rows_of(x, 0)).then_inc(x_in[0], 16)
            for dst, src in loads:
                sp.dma_start(dst, src).then_inc(w_in, 16)
            for g in range(1, XS):
                sp.dma_start(x_sb[:, g], rows_of(x, g)).then_inc(x_in[g], 16)

            def store(g, j):
                sp.wait_ge(y_ready, (g + 1) * 4)
                sp.dma_start(rows_of(out, g), y_sb[:, j % 2]).then_inc(y_out[j % 2], 16)

            def load(g, j):
                sp.dma_start(x_sb[:, j % XS], rows_of(x, g)).then_inc(x_in[j % XS], 16)

            with sp.Fori(0, (NG - 5) // XS) as q:
                for j in range(XS):
                    store(q * XS + j, j)
                    load(q * XS + j + XS, j)
            for g in range(NG - 5, NG - 1):
                store(g, g)
                if g + XS == NG - 1:
                    sp.dma_start(x_sb[0:TAIL_A, g % XS], tail_of(x, 0, TAIL_A)).then_inc(x_in[g % XS], 16)
                    sp.dma_start(x_sb[TAIL_A:TAIL_P, g % XS], tail_of(x, TAIL_A, TAIL_P)).then_inc(x_in[g % XS], 16)
            sp.wait_ge(y_ready, NG * 4)
            s = (NG - 1) % 2
            sp.dma_start(tail_of(out, 0, TAIL_A), y_sb[0:TAIL_A, s]).then_inc(y_out[s], 16)
            sp.dma_start(tail_of(out, TAIL_A, TAIL_P), y_sb[TAIL_A:TAIL_P, s]).then_inc(y_out[s], 16)

            def edge_load(c, j, gathered=None):
                s = j % 2
                if gathered is not None:
                    sp.wait_ge(xg_in[s], gathered)
                sp.dma_start(dst_sb[:, s], dst_cols[c]).then_inc(dst_in[s], 16)
                if gathered is not None:
                    sp.wait_ge(taken, 7 * (c - 1))
                    sp.wait_ge(row_ready, c - 1)
                sp.dma_start(src_sb[:, s], src_cols[c]).then_inc(src_in[s], 16)
                sp.dma_start(src_row[:, s], src_rows[c].partition_broadcast(P)).then_inc(src_in[s], 16)
                for b in range(4):
                    sp.dma_start(attr[32 * b:32 * b + 32, s], attr_t[c, b].partition_broadcast(32)).then_inc(attr_in[s], 16)

            edge_load(0, 0)
            edge_load(1, 1)
            with sp.Fori(1, (NC - 1) // 2) as m:
                edge_load(2 * m, 0, 64 * m)
                edge_load(2 * m + 1, 1, 64 * m)
            edge_load(NC - 1, 0, 64 * (NC // 2))
            sp.wait_ge(added, 16 * (1 + TPC * NC))

        @block.tensor
        def _(pe):
            pe.wait_ge(w_in, 16 * N_W)
            for rows, o in ((slice(0, P), bank[4]), (slice(P, D + 1), bank[5])):
                m = rows.stop - rows.start
                nc.tensor.matmul(o[0:m, 0:D], wmT_a[:, rows], wub_a[:], start=True, stop=False)
                nc.tensor.matmul(o[0:m, 0:D], wmT_b[:, rows], wub_b[:], start=False, stop=True).then_inc(wc_mm, 1)
            pe.wait_ge(w_ready, 8)

            def node_group(g, j, first=False):
                s = j % 2
                for half in range(2):
                    pe.wait_ge(h_ready, 2 * g + half + 1)
                    if not first:
                        pe.wait_ge(hT_ready, 2 * g + half - 1)
                    ta, tb = bank[half], bank[2 + half]
                    for pair in range(2):
                        h2 = hn[:, s, 2 * half + pair]
                        nc.tensor.transpose(ta[:, 2 * pair * P:2 * pair * P + P], h2[:, 0:P], ident[:])
                        nc.tensor.transpose(ta[:, 2 * pair * P + P:2 * pair * P + 2 * P], h2[:, 2 * P:3 * P], ident[:])
                        last = nc.tensor.transpose(tb[:, pair * P:pair * P + P], h2[:, P:2 * P], ident[:])
                    last.then_inc(hT_full, 1)
                for half in range(2):
                    pe.wait_ge(hT_ready, 2 * g + half + 1)
                    for t in range(2):
                        b = 2 * half + t
                        if not first:
                            pe.wait_ge(y_ready, 4 * g + b - 3)
                        o = bank[4 + b]
                        for pair in range(2):
                            tt, k0 = 2 * pair + t, 64 * t
                            nc.tensor.matmul(o[:, pair * D:pair * D + D], hT_a[:, half, tt * P:tt * P + P], wut_a[:, t],
                                             start=(pair == 0), stop=False, skip_group_check=True)
                            last = nc.tensor.matmul(
                                o[:, pair * D:pair * D + D], hT_b[k0:k0 + 64, half, pair * P:pair * P + P],
                                wut_b[k0:k0 + 64, :], start=False, stop=(pair == 1), skip_group_check=True)
                        last.then_inc(out_full, 1)

            node_group(0, 0, first=True)
            with pe.Fori(0, (NG - 1) // 2) as q:
                node_group(2 * q + 1, 1)
                node_group(2 * q + 2, 2)

            pe.wait_ge(y_ready, 4 * NG)

            def block_at(pos):
                return bank[pos % 4]

            def front_x(k, s, pos, of):
                for t in range(TPC):
                    last = nc.tensor.transpose(block_at(pos)[:, t * P:t * P + P], of(s, t), ident[:])
                last.then_inc(front_full, 1)

            def front_y(pos, j):
                nc.tensor.matmul(block_at(pos)[:], w3_sb[:, j, :], xsT[:], start=True, stop=True).then_inc(front_full, 1)

            def tp_slot(s, t, c0, c1):
                return bank[4 + 2 * s + t // 2][:, (t % 2) * D + c0:(t % 2) * D + c1]

            def products(s, parts, first=False, full=None):
                for t in range(TPC):
                    for n, (lhs, w, c0, c1) in enumerate(parts):
                        last = nc.tensor.matmul(tp_slot(s, t, c0, c1), lhs(t), w,
                                                start=first and t % 2 == 0 and n == 0,
                                                stop=full is not None and t % 2 == 1 and n == len(parts) - 1,
                                                skip_group_check=True)
                    if full is not None and t % 2 == 1:
                        last.then_inc(full, 1)
                return last

            def cols(buf):
                return lambda t: buf[:, t * P:t * P + P]

            def m_s1(s, h, first=False):
                products(s, [(cols(p_xs[:, h, j]), w1_sb[:, 2 * h + j, :], 0, MUL0) for j in range(2)], first)

            def m_v2(s, i):
                products(s, [(cols(p_v2[:, i, j]), w4_sb[:, j, :], MUL0 + 32 * i, MUL0 + 32 * i + 32) for j in range(2)])

            def m_d(s):
                products(s, [(cols(d_sum[:, j]), w2_sb[:, j, :], 0, MUL0) for j in range(2)]).then_inc(d_used, 1)

            def m_v(s):
                products(s, [(cols(v_sum[:, i]), deltas[:], MUL0 + 32 * i, MUL0 + 32 * i + 32) for i in range(3)],
                         full=tp_full)

            def merge(pos, half):
                o = block_at(pos)
                for u in range(2):
                    t = 2 * half + u
                    nc.tensor.matmul(o[:, u * P:u * P + P], tp_sb[:, t, 0:P], equal[:, t, :],
                                     start=(u == 0), stop=False, skip_group_check=True)
                    last = nc.tensor.matmul(o[0:D - P + 1, 256 + u * P:256 + u * P + P], tp_sb[:, t, P:D + 1],
                                            equal[:, t, :], start=False, stop=(u == 1), skip_group_check=True)
                last.then_inc(back_full, 1)

            def message(pos, half):
                o = block_at(pos)
                for u in range(2):
                    nc.tensor.matmul(o[:, u * D:u * D + D], tT_a[:, half, u * P:u * P + P], wc_a[:],
                                     start=(u == 0), stop=False, skip_group_check=True)
                    last = nc.tensor.matmul(o[:, u * D:u * D + D], tT_b[:, half, u * P:u * P + P], wc_b[:],
                                            start=False, stop=(u == 1), skip_group_check=True)
                last.then_inc(back_full, 1)

            def edge_chunk(k, j, front=True, back=True):
                s = j % 2
                if front:
                    pe.wait_ge(g_h, k + 1)
                    if back:
                        pe.wait_ge(taken, 7 * k - 3)
                        pe.wait_ge(tT_ready, 2 * k)
                    for t in range(TPC):
                        last = nc.tensor.transpose(block_at(0)[:, t * P:t * P + P], hg_scalars(s, t), ident[:])
                    last.then_inc(front_full, 1)
                    if back:
                        pe.wait_ge(taken, 7 * k)
                    front_x(k, s, 1, lambda s, t: hg_block(s, t, 0))
                    if back:
                        pe.wait_ge(msg_ready, 2 * k - 1)
                    front_x(k, s, 2, lambda s, t: hg_block(s, t, 1))
                if back:
                    pe.wait_ge(d_ready, k)
                    m_d(1 - s)
                if front:
                    if back:
                        pe.wait_ge(msg_ready, 2 * k)
                    front_x(k, s, 3, lambda s, t: hg_block(s, t, 2))
                if back:
                    pe.wait_ge(v_ready, k)
                    m_v(1 - s)
                if front:
                    pe.wait_ge(taken, 7 * k + 1)
                    if back:
                        pe.wait_ge(tp_ready, 2 * k)
                    m_s1(s, 0, first=True)
                    pe.wait_ge(xsT_ready, k + 1)
                    front_x(k, s, 4, lambda s, t: hg_block(s, t, 3))
                    pe.wait_ge(taken, 7 * k + 2)
                    m_s1(s, 1)
                    front_x(k, s, 5, lambda s, t: hg_block(s, t, 4))
                    pe.wait_ge(taken, 7 * k + 3)
                    m_v2(s, 0)
                if back:
                    pe.wait_ge(tp_ready, 2 * k + 1)
                    pe.wait_ge(eq_ready, k)
                    merge(6, 0)
                if front:
                    front_y(7, 0)
                    pe.wait_ge(taken, 7 * k + 4)
                    m_v2(s, 1)
                if back:
                    pe.wait_ge(tp_ready, 2 * k + 2)
                    merge(8, 1)
                if front:
                    pe.wait_ge(taken, 7 * k + 5)
                    front_y(9, 1)
                if back:
                    pe.wait_ge(tT_ready, 2 * k + 1)
                    message(10, 0)
                if front:
                    m_v2(s, 2)
                    pe.wait_ge(taken, 7 * k + 6)
                if back:
                    pe.wait_ge(tT_ready, 2 * k + 2)
                    message(11, 1)

            edge_chunk(0, 0, back=False)
            with pe.Fori(0, (NC - 1) // 2) as m:
                edge_chunk(2 * m + 1, 1)
                edge_chunk(2 * m + 2, 2)
            edge_chunk(NC, NC, front=False)

        @block.scalar
        def _(act):
            act.wait_ge(w_in, 16 * N_W)
            nc.scalar.activation(w1_sb[:], w1_raw[:], ACT.Copy, scale=float(C_S1)).then_inc(w_ready, 1)
            nc.scalar.activation(w2_sb[:], w2_raw[:], ACT.Copy, scale=float(C_S2)).then_inc(w_ready, 1)
            nc.scalar.activation(w3_sb[:], w3_raw[:], ACT.Copy, scale=float(C_V1)).then_inc(w_ready, 1)
            nc.scalar.activation(w4_sb[:], w4_raw[:], ACT.Copy, scale=float(C_V2)).then_inc(w_ready, 1)
            act.wait_ge(wc_mm, 2)
            nc.scalar.activation(wc_a[:], bank[4][:, 0:D], ACT.Copy).then_inc(w_ready, 1)
            nc.scalar.activation(wc_b[:], bank[5][0:D - P + 1, 0:D], ACT.Copy).then_inc(w_ready, 1)

            def node_sqrt(g):
                act.wait_ge(mv_ready, g + 1)
                nc.scalar.activation(std[:], mv[:, :, 1], ACT.Sqrt, bias=eps_ap[:]).then_inc(std_ready, 1)

            def node_norm(g, j, first=False):
                s = j % 2
                act.wait_ge(norm_ready, g + 1)
                for t in range(RPP):
                    at = 224 * (t % 2)
                    last = nc.scalar.activation(hn[:, s, t // 2, at:at + D], x_sb[:, j % XS, t], ACT.Relu,
                                                bias=nbias[:, s, t:t + 1], scale=rstd[:, s, t:t + 1])
                    if t % 4 == 3:
                        last.then_inc(h_ready, 1)

            def node_evac(g, j, first=False):
                for half in range(2):
                    act.wait_ge(hT_full, 2 * g + half + 1)
                    if not first:
                        act.wait_ge(out_full, 4 * g - 2 + 2 * half)
                    nc.scalar.activation(hT_a[:, half], bank[half][:], ACT.Copy)
                    nc.scalar.activation(hT_b[:, half], bank[2 + half][:, 0:256], ACT.Copy).then_inc(hT_ready, 1)

            act.wait_ge(prep, 2)
            node_sqrt(0)
            node_norm(0, 0)
            node_evac(0, 0, first=True)
            with act.Fori(0, (NG - 1) // 4) as q:
                for j in range(1, 5):
                    node_sqrt(4 * q + j)
                    node_norm(4 * q + j, j)
                    node_evac(4 * q + j, j)

            def edge_sqrt(c):
                act.wait_ge(g_mv, c + 1)
                nc.scalar.activation(std[:, 0:TPC], mv[:, 0:TPC, 1], ACT.Sqrt, bias=eps_ap[:]).then_inc(g_std, 1)

            def edge_norm(c, j, free=True):
                s = j % 2
                act.wait_ge(g_norm, c + 1)
                if free:
                    act.wait_ge(front_full, 8 * c - 10)
                for t in range(TPC):
                    norm = dict(bias=nbias[:, s, t:t + 1], scale=rstd[:, s, t:t + 1])
                    sc = xg[:, s, t, 0:MUL0].rearrange("p (n a) -> p n a", n=2)
                    vc = xg[:, s, t, MUL0:D].rearrange("p (a i) -> p i a", i=3)
                    nc.scalar.activation(hg[:, s, t, 0:2], sc.unsqueeze(2).broadcast_to([P, 2, 4, 32]), ACT.Relu, **norm)
                    last = nc.scalar.activation(hg[:, s, t, 2:5], vc.unsqueeze(2).broadcast_to([P, 3, 4, 32]), ACT.Relu, **norm)
                last.then_inc(g_h, 1)

            def edge_chunk(k, j, front=True, back=True, ahead=True):
                s, z = j % 2, (j + 1) % 2
                if front:
                    act.wait_ge(front_full, 8 * k + 1)
                    if back:
                        act.wait_ge(front_full, 8 * k)
                    nc.scalar.activation(xsT[:], bank[0][0:MUL0, :], ACT.Copy).then_inc(xsT_ready, 1)
                if back:
                    for half in range(2):
                        act.wait_ge(tp_full, 2 * k + half - 1)
                        nc.scalar.activation(
                            tp_sb[:, 2 * half:2 * half + 2, 0:D],
                            bank[4 + 2 * z + half][:, 0:2 * D].rearrange("p (t d) -> p t d", t=2),
                            ACT.Copy).then_inc(tp_ready, 1)
                if ahead:
                    edge_sqrt(k + 1)
                if back:
                    act.wait_ge(back_full, 4 * k - 3)
                    nc.scalar.activation(tT_a[:, 0], bank[2][:, 0:256], ACT.Copy)
                    nc.scalar.activation(tT_b[:, 0], bank[2][0:D - P + 1, 256:512], ACT.Copy).then_inc(tT_ready, 1)
                if ahead:
                    edge_norm(k + 1, j + 1, free=back)
                if back:
                    act.wait_ge(back_full, 4 * k - 2)
                    nc.scalar.activation(tT_a[:, 1], bank[0][:, 0:256], ACT.Copy)
                    nc.scalar.activation(tT_b[:, 1], bank[0][0:D - P + 1, 256:512], ACT.Copy).then_inc(tT_ready, 1)
                    for half in range(2):
                        act.wait_ge(back_full, 4 * k - 1 + half)
                        if half == 0:
                            act.wait_ge(msg_free, k)
                            act.wait_ge(row_ready, k)
                            nc.scalar.activation(row_i[:, z], row_f[:, z], ACT.Copy)
                        nc.scalar.activation(
                            msg[:, z, 2 * half:2 * half + 2], bank[2 + half][:, 0:2 * D].rearrange("p (t d) -> p t d", t=2),
                            ACT.Copy).then_inc(msg_ready, 1)

            act.sem_inc(tp_ready, 2)
            act.sem_inc(tT_ready, 2)
            act.sem_inc(msg_ready, 2)
            edge_sqrt(0)
            edge_norm(0, 0, free=False)
            edge_chunk(0, 0, back=False)
            with act.Fori(0, (NC - 3) // 2) as m:
                edge_chunk(2 * m + 1, 1)
                edge_chunk(2 * m + 2, 2)
            edge_chunk(NC - 2, NC - 2)
            edge_chunk(NC - 1, NC - 1, ahead=False)
            edge_chunk(NC, NC, front=False, ahead=False)

        @block.vector
        def _(dve):
            nc.vector.memset(wut_raw_b[:], 0.0)
            nc.vector.memset(eye_b[:], 0.0).then_inc(prep, 1)
            nc.vector.memset(eps_ap[:], EPS)
            nc.vector.memset(tp_sb[:, :, D:D + 1], 1.0)
            nc.vector.memset(zero_rows[:], 0.0)
            pads = hn[:, :, :, D:D + 64].rearrange("p s n (a b) -> p (s n) a b", a=2)
            nc.vector.memset(pads[:, :, :, 1:32], 0.0)
            nc.vector.memset(pads[:, :, :, 0:1], 1.0).then_inc(prep, 1)
            dve.wait_ge(w_in, 16 * N_W)
            nc.vector.tensor_tensor(wut_a[:], wut_raw_a[:], eye_a[:], ALU.add).then_inc(w_ready, 1)
            nc.vector.tensor_tensor(wut_b[:], wut_raw_b[:], eye_b[:], ALU.add).then_inc(w_ready, 1)

            def newton(var, mean, s, n, std_sem, value, step, step0, done):
                dve.wait_ge(std_sem, value)
                nc.vector.reciprocal(r0[:, 0:n], std[:, 0:n]).then_inc(step, 1)
                dve.wait_ge(step, step0 + 1)
                nc.vector.scalar_tensor_tensor(r1[:, 0:n], var, EPS, r0[:, 0:n], ALU.add, ALU.mult).then_inc(step, 1)
                dve.wait_ge(step, step0 + 2)
                nc.vector.scalar_tensor_tensor(r2[:, 0:n], r1[:, 0:n], -0.5, r0[:, 0:n], ALU.mult, ALU.mult).then_inc(step, 1)
                dve.wait_ge(step, step0 + 3)
                nc.vector.scalar_tensor_tensor(rstd[:, s, 0:n], r2[:, 0:n], 1.5, r0[:, 0:n], ALU.add, ALU.mult).then_inc(step, 1)
                dve.wait_ge(step, step0 + 4)
                nc.vector.scalar_tensor_tensor(nbias[:, s, 0:n], mean, -1.0, rstd[:, s, 0:n], ALU.mult, ALU.mult).then_inc(done, 1)

            def node_stats(g, j, arrived):
                s = j % 2
                dve.wait_ge(x_in[j % XS], arrived)
                for t in range(RPP):
                    last = nc.vector.bn_stats(bst[:, t], x_sb[:, j % XS, t])
                last.then_inc(stats_done, 1)
                dve.wait_ge(stats_done, g + 1)
                dve.sem_inc(passed_dve, 1)
                for t in range(RPP):
                    last = nc.vector.bn_aggr(mv[:, t], bst[:, t])
                last.then_inc(mv_ready, 1)

            def node_newton(g, j):
                newton(mv[:, :, 1], mv[:, :, 0], j % 2, RPP, std_ready, g + 1, rstd_step, 4 * g, norm_ready)

            def node_add(g, j, y_free=None):
                s = j % 2
                if y_free is not None:
                    dve.wait_ge(y_out[s], y_free)
                for b in range(4):
                    dve.wait_ge(out_full, 4 * g + b + 1)
                    r0_, r1_ = 4 * (b // 2) + b % 2, 4 * (b // 2) + 4
                    nc.vector.tensor_tensor(
                        y_sb[:, s, r0_:r1_:2], bank[4 + b][:, 0:2 * D].rearrange("p (t d) -> p t d", t=2),
                        x_sb[:, j % XS, r0_:r1_:2], ALU.add).then_inc(y_ready, 1)

            node_stats(0, 0, 16)
            node_newton(0, 0)
            for g in range(2):
                node_stats(g + 1, g + 1, 16)
                node_newton(g + 1, g + 1)
                node_add(g, g)
            with dve.Fori(0, (NG - 5) // 4) as q:
                for j in range(2, 6):
                    g = 4 * q + j
                    node_stats(g + 1, j + 1, 16 * q + 16 * ((j + 1) // XS) + 16)
                    node_newton(g + 1, j + 1)
                    node_add(g, j, 32 * q + 16 * (j // 2))
            for g in range(NG - 3, NG):
                if g + 1 < NG:
                    node_stats(g + 1, g + 1, 16 * ((g + 1) // XS + 1) + 16 * (g + 1 == NG - 1))
                    node_newton(g + 1, g + 1)
                node_add(g, g, 16 * (g // 2))

            def edge_stats(c, j, arrived):
                dve.wait_ge(xg_in[j % 2], arrived)
                for t in range(TPC):
                    last = nc.vector.bn_stats(bst[:, t], xg[:, j % 2, t])
                last.then_inc(g_stats, 1)
                dve.wait_ge(g_stats, c + 1)
                dve.sem_inc(passed_dve, 1)
                for t in range(TPC):
                    last = nc.vector.bn_aggr(mv[:, t], bst[:, t])
                last.then_inc(g_mv, 1)

            def edge_newton(c, j):
                newton(mv[:, 0:TPC, 1], mv[:, 0:TPC, 0], j % 2, TPC, g_std, c + 1, g_step, 4 * c, g_norm)

            def times(o, pos, a):
                n = a.shape[1]
                return nc.vector.tensor_tensor(o, bank[pos % 4][:].unsqueeze(1).broadcast_to([P, n, CHUNK]), a, ALU.mult)

            def edge_chunk(k, j, arrived, arrived2, prev=True, ahead=True):
                s = j % 2
                dve.wait_ge(attr_in[s], 4 * arrived)
                for h in range(2):
                    dve.wait_ge(front_full, 8 * k + 2 + h)
                    times(p_xs[:, h], 1 + h, attr[:, s, 0:2]).then_inc(taken, 1)
                for i in range(3):
                    dve.wait_ge(front_full, 8 * k + 4 + i)
                    times(p_v2[:, i], 3 + i, attr[:, s, 0:2])
                    if prev and i == 0:
                        dve.wait_ge(d_ready, k)
                    times(p_d[:, i], 3 + i, attr[:, s, 2 + 2 * i:4 + 2 * i]).then_inc(taken, 1)
                    if ahead and i == 0:
                        edge_stats(k + 1, j + 1, arrived2)
                    if ahead and i == 1:
                        edge_newton(k + 1, j + 1)
                if prev:
                    dve.wait_ge(v_ready, k)
                for u, pos in ((0, 7), (1, 9)):
                    dve.wait_ge(front_full, 8 * k + 7 + u)
                    times(p_y[:, u], pos, attr[:, s, 2 + u:8:2]).then_inc(taken, 1)
                dve.wait_ge(src_in[s], 2 * arrived)
                nc.vector.tensor_copy(src_f[:], src_sb[:, s]).then_inc(eq_step, 1)
                dve.wait_ge(eq_step, 4 * k + 1)
                if prev:
                    dve.wait_ge(back_full, 4 * k - 2)
                for t in range(TPC):
                    nc.vector.scalar_tensor_tensor(
                        scrap[:, t], src_row[:, s, t * P:t * P + P], src_f[:, t:t + 1], before[:],
                        ALU.is_equal, ALU.mult, accum_out=n_before[:, t:t + 1])
                    last = nc.vector.tensor_scalar(equal[:, t], src_row[:, s, t * P:t * P + P], src_f[:, t:t + 1],
                                                   None, ALU.is_equal)
                last.then_inc(eq_ready, 1)
                nc.vector.tensor_scalar(to_spare[:], src_f[:], -1.0, spare_row[:], ALU.mult, ALU.add).then_inc(eq_step, 1)
                dve.wait_ge(eq_ready, k + 1)
                dve.wait_ge(eq_step, 4 * k + 2)
                nc.vector.scalar_tensor_tensor(shift[:], n_before[:], 0.5, to_spare[:], ALU.is_gt, ALU.mult).then_inc(eq_step, 2)
                dve.wait_ge(eq_step, 4 * k + 4)
                nc.vector.tensor_tensor(row_f[:, s], shift[:], src_f[:], ALU.add).then_inc(row_ready, 1)

            edge_stats(0, 0, 64)
            edge_newton(0, 0)
            edge_chunk(0, 0, 16, 64, prev=False)
            with dve.Fori(0, (NC - 3) // 2) as m:
                edge_chunk(2 * m + 1, 1, 16 * m + 16, 64 * m + 128)
                edge_chunk(2 * m + 2, 2, 16 * m + 32, 64 * m + 128)
            n = NC // 2
            edge_chunk(NC - 2, NC - 2, 16 * n, 64 * n + 64)
            edge_chunk(NC - 1, NC - 1, 16 * n + 16, 0, ahead=False)

        @block.gpsimd
        def _(pool):
            pool.wait_ge(prep, 2)
            pool.sem_inc(msg_free, 3)
            pool.dma_start(out[N_NODES:OUT_ROWS, :], zero_rows[:]).then_inc(added, 16)

            def gather(s, t):
                nc.gpsimd.indirect_dma_start(
                    out=xg[:, s, t], out_offset=None, in_=x,
                    in_offset=bass.IndirectOffsetOnAxis(ap=dst_sb[:, s, t:t + 1], axis=0)).then_inc(xg_in[s], 16)

            def scatter(k2, s, t):
                if t == 0:
                    pool.wait_ge(msg_ready, 2 * k2 + 3)
                if t == 2:
                    pool.wait_ge(msg_ready, 2 * k2 + 4)
                pool.wait_ge(added, 64 * k2 + 16 * t + 16)
                pool.sem_inc(passed_pool, 1)
                nc.gpsimd.indirect_dma_start(
                    out=out, out_offset=bass.IndirectOffsetOnAxis(ap=row_i[:, s, t:t + 1], axis=0),
                    in_=msg[:, s, t], in_offset=None, compute_op=ALU.add).then_inc(added, 16)

            def edge_chunk(k, j, arrived, gathers=True, sums=True, scatters=True):
                s, z = j % 2, (j + 1) % 2
                if gathers:
                    pool.wait_ge(dst_in[z], arrived)
                    if not (isinstance(k, int) and k == 0):
                        pool.wait_ge(g_h, k)
                if scatters:
                    scatter(k - 2, s, 0)
                if gathers:
                    gather(z, 0)
                    gather(z, 1)
                if scatters:
                    scatter(k - 2, s, 1)
                if gathers:
                    gather(z, 2)
                    gather(z, 3)
                if sums:
                    pool.wait_ge(taken, 7 * k + 4)
                    if not (isinstance(k, int) and k == 0):
                        pool.wait_ge(d_used, k)
                    nc.gpsimd.tensor_tensor(d_part[:], p_d[:, 0], p_d[:, 1], ALU.add).then_inc(d_part_ready, 1)
                if scatters:
                    scatter(k - 2, s, 2)
                if sums:
                    pool.wait_ge(taken, 7 * k + 5)
                    pool.wait_ge(d_part_ready, k + 1)
                    nc.gpsimd.tensor_tensor(d_sum[:], d_part[:], p_d[:, 2], ALU.add).then_inc(d_ready, 1)
                if scatters:
                    scatter(k - 2, s, 3)
                    pool.wait_ge(added, 64 * k - 48)
                    pool.sem_inc(msg_free, 1)
                if sums:
                    pool.wait_ge(taken, 7 * k + 7)
                    if not (isinstance(k, int) and k == 0):
                        pool.wait_ge(tp_full, 2 * k)
                    nc.gpsimd.tensor_tensor(v_sum[:], p_y[:, 0], p_y[:, 1], ALU.add).then_inc(v_ready, 1)

            pool.wait_ge(dst_in[0], 16)
            for t in range(TPC):
                gather(0, t)
            edge_chunk(0, 0, 16, scatters=False)
            edge_chunk(1, 1, 32, scatters=False)
            pool.wait_ge(y_out[0], 16 * ((NG + 1) // 2) + 16)
            pool.wait_ge(y_out[1], 16 * (NG // 2))
            with pool.Fori(0, (NC - 3) // 2) as m:
                edge_chunk(2 * m + 2, 2, 16 * m + 32)
                edge_chunk(2 * m + 3, 3, 16 * m + 48)
            edge_chunk(NC - 1, NC - 1, 0, gathers=False)
            edge_chunk(NC, NC, 0, gathers=False, sums=False)
            edge_chunk(NC + 1, NC + 1, 0, gathers=False, sums=False)


def kernel(**inputs):
    import numpy as _np
    import concourse.bacc as _bacc
    from concourse import mybir as _mybir
    from concourse.bass_utils import run_bass_kernel_spmd as _run

    get = lambda n: _np.ascontiguousarray(inputs[n])
    pad = E_PAD - N_EDGES
    dst = _np.concatenate([get("dst"), _np.zeros(pad, _np.int32)])
    src = _np.concatenate([get("src"), (N_NODES + _np.arange(N_EDGES, E_PAD) % P).astype(_np.int32)])
    attr = _np.concatenate([get("edge_attr_32"), _np.zeros((pad, DE), _np.float32)])
    order = _np.array([[MB * kind and (MB + 3 * b + kind - 1) or b for kind in range(4) for b in (4 * 0 + b4, 4 + b4)]
                       for b4 in range(4)])
    attr_t = attr[:, order.ravel()].reshape(NC, CHUNK, 4, 8).transpose(0, 2, 3, 1)
    hid = _np.concatenate([_np.arange(MUL0)] + [MUL0 + i + 3 * _np.arange(MUL1) for i in range(3)])
    w1, w2, w3, w4 = (get(f"L0_gnn_W{i}") for i in (1, 2, 3, 4))
    wm, wu = get("L0_gnn_Wm"), get("L0_gnn_Wu")
    eye = _np.eye(D, dtype=_np.float32)
    arrays = {
        "x": get("x"),
        "dst_cols": dst.reshape(NC, TPC, P).transpose(0, 2, 1),
        "src_cols": src.reshape(NC, TPC, P).transpose(0, 2, 1),
        "src_rows": src.reshape(NC, CHUNK),
        "attr_t": attr_t,
        "w1": w1.reshape(2, 32, 2, 4, MUL0).transpose(3, 1, 0, 2, 4).reshape(P, 4, MUL0),
        "w2": w2.reshape(32, 2, 4, MUL0).transpose(2, 0, 1, 3).reshape(P, 2, MUL0),
        "w3": w3.reshape(MUL0, 2, P),
        "w4": w4.reshape(32, 2, 4, MUL1).transpose(2, 0, 1, 3).reshape(P, 2, MUL1),
        "wm_t": wm[hid].T,
        "bm": get("L0_gnn_bm").reshape(D, 1),
        "wu_top": wu[:D], "wu_bot": wu[D:], "bu": get("L0_gnn_bu").reshape(1, D),
        "eye": eye[:P, :P], "eye160": eye,
        "delta": _np.tile(eye[:MUL1, :MUL1], (4, 1)),
        "earlier": _np.tril(_np.ones((P, P), _np.float32), -1),
        "spare": (N_NODES + _np.arange(P, dtype=_np.float32)).reshape(P, 1),
    }
    nc = _bacc.Bacc("TRN2", target_bir_lowering=False, num_devices=1)
    args = {}
    for name, a in arrays.items():
        arrays[name] = a = _np.ascontiguousarray(a)
        args[name] = nc.dram_tensor(name, a.shape, _mybir.dt.from_np(a.dtype), kind="ExternalInput").ap()
    out = nc.dram_tensor("out", (OUT_ROWS, D), _mybir.dt.float32, kind="ExternalOutput").ap()
    gnn_program(nc, *args.values(), out)
    got = _run(nc, [arrays], core_ids=[0]).results[0]["out"]
    return got[:N_NODES]
```

```python
import numpy as np
import concourse.bass as bass
from concourse import mybir
from contextlib import ExitStack

N_NODES, N_EDGES = 50000, 25000
D, DE = 160, 32
MUL0, MUL1, MB = 64, 32, 8
P = 128
EPS = 1e-5

RPP = 8
GROUP = P * RPP
NG = -(-N_NODES // GROUP)
TAIL_ROWS = N_NODES - (NG - 1) * GROUP
TAIL_P = TAIL_ROWS // RPP
TAIL_A = TAIL_P // 16 * 16
XS = 4

TPC = 4
CHUNK = TPC * P
NC = -(-N_EDGES // CHUNK)
E_PAD = NC * CHUNK
OUT_ROWS = N_NODES + P

C_S1 = 1.0 / np.sqrt(2.0) / np.sqrt(MUL0 * MB)
C_S2 = 1.0 / np.sqrt(2.0) / (np.sqrt(3.0) * np.sqrt(MUL1 * MB))
C_V1 = 1.0 / np.sqrt(2.0) / np.sqrt(MUL0 * MB)
C_V2 = 1.0 / np.sqrt(2.0) / np.sqrt(MUL1 * MB)


def gnn_program(nc, x, dst_cols, src_cols, src_rows, attr_t, w1, w2, w3, w4, wm_bm_t, wu_top_a, wu_top_b,
                wu_bot, eye, delta, earlier, spare, out):
    f32, i32 = mybir.dt.float32, mybir.dt.int32
    ALU, ACT = mybir.AluOpType, mybir.ActivationFunctionType
    ctx = ExitStack()

    def sb(name, shape, dt=f32):
        return ctx.enter_context(nc.sbuf_tensor(name, shape, dt))

    def sem(name):
        return ctx.enter_context(nc.semaphore(name))

    with ctx:
        bank = [ctx.enter_context(nc.psum_tensor(f"bank{i}", [P, 512], f32)) for i in range(8)]

        ident = sb("ident", [P, P])
        deltas = sb("deltas", [P, MUL1])
        before = sb("before", [P, P])
        spare_row = sb("spare_row", [P, 1])
        w1_raw, w1_sb = sb("w1_raw", [P, 4, MUL0]), sb("w1_sb", [P, 4, MUL0])
        w2_raw, w2_sb = sb("w2_raw", [P, 2, MUL0]), sb("w2_sb", [P, 2, MUL0])
        w3_raw, w3_sb = sb("w3_raw", [MUL0, 2, P]), sb("w3_sb", [MUL0, 2, P])
        w4_raw, w4_sb = sb("w4_raw", [P, 2, MUL1]), sb("w4_sb", [P, 2, MUL1])
        wmT_a, wmT_b = sb("wmT_a", [P, D + 1]), sb("wmT_b", [D - P, D + 1])
        wub_a, wub_b = sb("wub_a", [P, D]), sb("wub_b", [D - P, D])
        wc_s, wc_v = sb("wc_s", [P, D]), sb("wc_v", [3 * MUL1 + 1, D])
        wut_a, wut_b = sb("wut_a", [P, 2, D]), sb("wut_b", [P, D])
        eps_ap = sb("eps_ap", [P, 1])

        x_sb = sb("x_sb", [P, XS, RPP, D])
        y_sb = sb("y_sb", [P, 2, RPP, D])
        hn = sb("hn", [P, 2, RPP // 2, 384])
        hT_a, hT_b = sb("hT_a", [P, 2, 512]), sb("hT_b", [P, 2, 256])
        bst = sb("bst", [P, RPP, 6])
        mv = sb("mv", [P, RPP, 2])
        std = sb("std", [P, RPP])
        r0, r1, r2 = sb("r0", [P, RPP]), sb("r1", [P, RPP]), sb("r2", [P, RPP])
        rstd = sb("rstd", [P, 2, RPP])
        nbias = sb("nbias", [P, 2, RPP])
        node_ln = (r0, r1, r2, rstd, nbias)

        dst_sb = sb("dst_sb", [P, 2, TPC], i32)
        src_sb = sb("src_sb", [P, 2, TPC], i32)
        src_f = sb("src_f", [P, TPC])
        src_row = sb("src_row", [P, 2, CHUNK], i32)
        attr = sb("attr", [P, 2, 8, CHUNK])
        xg = sb("xg", [P, 2, TPC, D])
        e_bst, e_mv, e_std = sb("e_bst", [P, TPC, 6]), sb("e_mv", [P, TPC, 2]), sb("e_std", [P, TPC])
        e_rstd, e_nbias = sb("e_rstd", [P, 2, TPC]), sb("e_nbias", [P, 2, TPC])
        edge_ln = (sb("e_r0", [P, TPC]), sb("e_r1", [P, TPC]), sb("e_r2", [P, TPC]), e_rstd, e_nbias)
        hg = sb("hg", [P, 2, TPC, 5, 4, 32])
        xsT = sb("xsT", [MUL0, CHUNK])
        xv2 = sb("xv2", [P, CHUNK])
        p_xs = sb("p_xs", [P, 2, 2, CHUNK])
        p_v2 = sb("p_v2", [P, 3, 2, CHUNK])
        p_d = sb("p_d", [P, 3, 2, CHUNK])
        p_y = sb("p_y", [P, 2, 3, CHUNK])
        equal = sb("equal", [P, 2, TPC, P])
        scrap = sb("scrap", [P, TPC, P])
        n_before = sb("n_before", [P, TPC])
        to_spare = sb("to_spare", [P, TPC])
        shift = sb("shift", [P, TPC])
        row_f = sb("row_f", [P, 2, TPC])
        row_i = sb("row_i", [P, 2, TPC], i32)
        tp_s = sb("tp_s", [P, CHUNK])
        tp_v = sb("tp_v", [3 * MUL1 + 1, CHUNK])
        raw_msg = sb("raw_msg", [P, TPC, D])
        msg = sb("msg", [P, 2, TPC, D])
        zero_rows = sb("zero_rows", [P, D])

        w_in, w_in2 = sem("w_in"), sem("w_in2")
        wut_ready = sem("wut_ready")
        w_ready = sem("w_ready")
        wc_mm = sem("wc_mm")
        x_in = [sem(f"x_in{s}") for s in range(XS)]
        y_out = [sem(f"y_out{s}") for s in range(2)]
        stats_done, mv_ready, std_ready = sem("stats_done"), sem("mv_ready"), sem("std_ready")
        rstd_step, norm_ready = sem("rstd_step"), sem("norm_ready")
        h_ready, hT_full, hT_ready, out_full, y_ready = (
            sem(n) for n in ("h_ready", "hT_full", "hT_ready", "out_full", "y_ready"))
        prep = sem("prep")
        dst_in = [sem(f"dst_in{s}") for s in range(2)]
        src_in = [sem(f"src_in{s}") for s in range(2)]
        attr_in = [sem(f"attr_in{s}") for s in range(2)]
        xg_in = [sem(f"xg_in{s}") for s in range(2)]
        g_stats, g_mv, g_std, g_step, g_norm, g_h = (
            sem(n) for n in ("g_stats", "g_mv", "g_std", "g_step", "g_norm", "g_h"))
        front_full, taken = sem("front_full"), sem("taken")
        s_full, v_full, raw_full, msg_full = (sem(n) for n in ("s_full", "v_full", "raw_full", "msg_full"))
        xsT_ready, xv2_ready, s_ready, v_ready, raw_ready, msg_ready = (
            sem(n) for n in ("xsT_ready", "xv2_ready", "s_ready", "v_ready", "raw_ready", "msg_ready"))
        pool_d1, pool_d = sem("pool_d1"), sem("pool_d")
        eq_ready, eq_step, row_ready = sem("eq_ready"), sem("eq_step"), sem("row_ready")
        spare_in = sem("spare_in")
        added = sem("added")
        msg_free = sem("msg_free")
        passed_dve, passed_pool = sem("passed_dve"), sem("passed_pool")

        block = ctx.enter_context(nc.Block())

        def bcast(ap, shape):
            return ap.broadcast_to(shape)

        def hg_block(s, t, n):
            return hg[:, s, t, n].rearrange("p b a -> p (b a)")

        def hg_scalars(s, t):
            return hg[:, s, t].rearrange("p n b a -> p (n b a)")[:, 96:96 + P]

        def rows_of(dram, g):
            return dram[bass.ds(g * GROUP, GROUP), :].rearrange("(p r) d -> p r d", r=RPP)

        TB = (NG - 1) * GROUP

        def tail_of(dram, p0, p1):
            return dram[TB + p0 * RPP:TB + p1 * RPP, :].rearrange("(p r) d -> p r d", r=RPP)

        def newton(eng, ns, var, mean, s, std, ln, std_sem, value, step, step0, done):
            r0, r1, r2, rstd, nbias = ln
            eng.wait_ge(std_sem, value)
            nc.vector.reciprocal(r0[:], std[:]).then_inc(step, 1)
            eng.wait_ge(step, step0 + 1)
            ns.scalar_tensor_tensor(r1[:], var, EPS, r0[:], ALU.add, ALU.mult).then_inc(step, 1)
            eng.wait_ge(step, step0 + 2)
            ns.scalar_tensor_tensor(r2[:], r1[:], -0.5, r0[:], ALU.mult, ALU.mult).then_inc(step, 1)
            eng.wait_ge(step, step0 + 3)
            ns.scalar_tensor_tensor(rstd[:, s], r2[:], 1.5, r0[:], ALU.add, ALU.mult).then_inc(step, 1)
            eng.wait_ge(step, step0 + 4)
            ns.scalar_tensor_tensor(nbias[:, s], mean, -1.0, rstd[:, s], ALU.mult, ALU.mult).then_inc(done, 1)

        N_W, N_W2 = 3, 11

        @block.sync
        def _(sp):
            node_loads = [(ident[:], eye), (wut_a[:], wu_top_a), (wut_b[:], wu_top_b)]
            edge_loads = [
                (deltas[:], delta), (before[:], earlier), (spare_row[:], spare),
                (w1_raw[:], w1), (w2_raw[:], w2), (w3_raw[:], w3), (w4_raw[:], w4),
                (wmT_a[:], wm_bm_t[0:P, :]), (wmT_b[:], wm_bm_t[P:D, :]),
                (wub_a[:], wu_bot[0:P, :]), (wub_b[:], wu_bot[P:D, :]),
            ]
            assert len(node_loads) == N_W and len(edge_loads) == N_W2
            sp.dma_start(x_sb[:, 0], rows_of(x, 0)).then_inc(x_in[0], 16)
            for dst, src in node_loads:
                sp.dma_start(dst, src).then_inc(w_in, 16)
            for g in range(1, XS):
                sp.dma_start(x_sb[:, g], rows_of(x, g)).then_inc(x_in[g], 16)
            for dst, src in edge_loads:
                sp.dma_start(dst, src).then_inc(w_in2, 16)

            def edge_load(c, j, gathered=None, reused=True, paced=True):
                s, z = j % 2, (j + 1) % 2
                if gathered is not None:
                    sp.wait_ge(xg_in[z], gathered)
                    sp.dma_start(dst_sb[:, z], dst_cols[c + 1]).then_inc(dst_in[z], 16)
                if reused:
                    sp.wait_ge(row_ready, c - 1)
                sp.dma_start(src_sb[:, s], src_cols[c]).then_inc(src_in[s], 16)
                sp.dma_start(src_row[:, s], src_rows[c].partition_broadcast(P)).then_inc(src_in[s], 16)
                if reused:
                    sp.wait_ge(taken, 6 * (c - 1))
                    sp.wait_ge(pool_d, c - 1)
                for b in range(4):
                    if paced and b:
                        sp.wait_ge(added, 64 * (c - 3) + 16 * b + 16)
                    sp.dma_start(attr[32 * b:32 * b + 32, s], attr_t[c, b].partition_broadcast(32)).then_inc(attr_in[s], 16)

            for c in range(2):
                sp.dma_start(dst_sb[:, c], dst_cols[c]).then_inc(dst_in[c], 16)
            edge_load(0, 0, reused=False, paced=False)

            def store(g, j):
                sp.wait_ge(y_ready, (g + 1) * 4)
                sp.dma_start(rows_of(out, g), y_sb[:, j % 2]).then_inc(y_out[j % 2], 16)

            def load(g, j):
                sp.dma_start(x_sb[:, j % XS], rows_of(x, g)).then_inc(x_in[j % XS], 16)

            with sp.Fori(0, (NG - 5) // XS) as q:
                for j in range(XS):
                    store(q * XS + j, j)
                    load(q * XS + j + XS, j)
            for g in range(NG - 5, NG - 1):
                store(g, g)
                if g + XS == NG - 1:
                    sp.dma_start(x_sb[0:TAIL_A, g % XS], tail_of(x, 0, TAIL_A)).then_inc(x_in[g % XS], 16)
                    sp.dma_start(x_sb[TAIL_A:TAIL_P, g % XS], tail_of(x, TAIL_A, TAIL_P)).then_inc(x_in[g % XS], 16)
            sp.wait_ge(y_ready, NG * 4)
            s = (NG - 1) % 2
            sp.dma_start(tail_of(out, 0, TAIL_A), y_sb[0:TAIL_A, s]).then_inc(y_out[s], 16)
            sp.dma_start(tail_of(out, TAIL_A, TAIL_P), y_sb[TAIL_A:TAIL_P, s]).then_inc(y_out[s], 16)

            edge_load(1, 1, 64, reused=False, paced=False)
            edge_load(2, 2, 64, paced=False)
            with sp.Fori(0, (NC - 5) // 2) as m:
                edge_load(2 * m + 3, 3, 64 * m + 128)
                edge_load(2 * m + 4, 4, 64 * m + 128)
            edge_load(NC - 2, NC - 2, 64 * (NC // 2))
            edge_load(NC - 1, NC - 1)
            sp.wait_ge(added, 16 * (1 + TPC * NC))

        @block.tensor
        def _(pe):
            pe.wait_ge(wut_ready, 2)

            def transpose_half(n, s, half):
                pe.wait_ge(h_ready, n + 1)
                ta, tb = bank[half], bank[2 + half]
                for pair in range(2):
                    h2 = hn[:, s, 2 * half + pair]
                    nc.tensor.transpose(ta[:, 2 * pair * P:2 * pair * P + P], h2[:, 0:P], ident[:])
                    nc.tensor.transpose(ta[:, 2 * pair * P + P:2 * pair * P + 2 * P], h2[:, 2 * P:3 * P], ident[:])
                    last = nc.tensor.transpose(tb[:, pair * P:pair * P + P], h2[:, P:2 * P], ident[:])
                last.then_inc(hT_full, 1)

            def update_half(n, half, first=False):
                pe.wait_ge(hT_ready, n + 1)
                for t in range(2):
                    if not first:
                        pe.wait_ge(y_ready, 2 * n + t - 3)
                    o = bank[4 + 2 * half + t]
                    for pair in range(2):
                        tt, k0 = 2 * pair + t, 64 * t
                        nc.tensor.matmul(o[:, pair * D:pair * D + D], hT_a[:, half, tt * P:tt * P + P], wut_a[:, t],
                                         start=(pair == 0), stop=False, skip_group_check=True)
                        last = nc.tensor.matmul(
                            o[:, pair * D:pair * D + D], hT_b[k0:k0 + 64, half, pair * P:pair * P + P],
                            wut_b[k0:k0 + 64, :], start=False, stop=(pair == 1), skip_group_check=True)
                    last.then_inc(out_full, 1)

            def node_group(g, j):
                transpose_half(2 * g, j % 2, 0)
                update_half(2 * g - 1, 1)
                transpose_half(2 * g + 1, j % 2, 1)
                update_half(2 * g, 0)

            transpose_half(0, 0, 0)
            transpose_half(1, 0, 1)
            update_half(0, 0, first=True)
            transpose_half(2, 1, 0)
            update_half(1, 1, first=True)
            transpose_half(3, 1, 1)
            update_half(2, 0)
            with pe.Fori(0, (NG - 3) // 2) as q:
                node_group(2 * q + 2, 2)
                node_group(2 * q + 3, 3)
            node_group(NG - 1, NG - 1)
            update_half(2 * NG - 1, 1)

            def front_x(s, pos, n):
                for t in range(TPC):
                    lhs = hg_scalars(s, t) if n is None else hg_block(s, t, n)
                    last = nc.tensor.transpose(bank[pos % 4][:, t * P:t * P + P], lhs, ident[:])
                last.then_inc(front_full, 1)

            def front_y(pos, j):
                nc.tensor.matmul(bank[pos % 4][:], w3_sb[:, j, :], xsT[:], start=True, stop=True).then_inc(front_full, 1)

            def scalars(w, n, p, first=False, last=False):
                for j in range(2):
                    mm = nc.tensor.matmul(bank[4][MUL0 * j:MUL0 * j + MUL0, :], w[:, n(j), :], p[:, j, :],
                                          start=first, stop=last)
                if last:
                    mm.then_inc(s_full, 1)

            def vectors(w, p, first=False, last=False):
                for i in range(3):
                    mm = nc.tensor.matmul(bank[5][MUL1 * i:MUL1 * i + MUL1, :], w, p(i), start=first, stop=last)
                return mm

            def messages(half):
                for u in range(2):
                    t = 2 * half + u
                    nc.tensor.matmul(bank[6][:, u * D:u * D + D], tp_s[:, t * P:t * P + P], wc_s[:],
                                     start=(u == 0), stop=False, skip_group_check=True)
                    mm = nc.tensor.matmul(bank[6][:, u * D:u * D + D], tp_v[:, t * P:t * P + P], wc_v[:],
                                          start=False, stop=(u == 1), skip_group_check=True)
                mm.then_inc(raw_full, 1)

            def merge(half, z):
                for u in range(2):
                    t = 2 * half + u
                    mm = nc.tensor.matmul(bank[7][:, u * D:u * D + D], equal[:, z, t, :], raw_msg[:, t, :],
                                          start=(u == 0), stop=(u == 1), skip_group_check=True)
                mm.then_inc(msg_full, 1)

            def combine_weights():
                for rows, o, p0 in ((slice(0, MUL0), bank[6], 0), (slice(0, MUL0), bank[6], MUL0),
                                    (slice(MUL0, D + 1), bank[7], 0)):
                    p1 = p0 + rows.stop - rows.start
                    nc.tensor.matmul(o[p0:p1, 0:D], wmT_a[:, rows], wub_a[:], start=True, stop=False)
                    nc.tensor.matmul(o[p0:p1, 0:D], wmT_b[:, rows], wub_b[:], start=False, stop=True).then_inc(wc_mm, 1)

            def edge_chunk(k, j, front=True, back=True):
                s, z = j % 2, (j + 1) % 2
                if front:
                    pe.wait_ge(g_h, k + 1)
                    if back:
                        pe.wait_ge(taken, 6 * k - 2)
                    front_x(s, 0, None)
                    if back:
                        pe.wait_ge(xv2_ready, k)
                        pe.wait_ge(taken, 6 * k - 1)
                    front_x(s, 1, 0)
                    front_x(s, 2, 1)
                if back:
                    pe.wait_ge(pool_d1, k)
                    scalars(w2_sb, lambda j: j, p_d[:, 2], last=True)
                if front:
                    if back:
                        pe.wait_ge(taken, 6 * k)
                    front_x(s, 3, 2)
                if not back:
                    pe.wait_ge(y_ready, 4 * NG)
                    pe.wait_ge(w_in2, 16 * N_W2)
                    combine_weights()
                    pe.wait_ge(w_ready, 4)
                if back:
                    pe.wait_ge(taken, 6 * k)
                    pe.wait_ge(pool_d, k)
                    pe.wait_ge(v_ready, k)
                    vectors(deltas[:], lambda i: p_y[:, 0, i], first=True)
                    vectors(deltas[:], lambda i: p_y[:, 1, i])
                    vectors(w4_sb[:, 0, :], lambda i: p_v2[:, i, 0])
                    vectors(w4_sb[:, 1, :], lambda i: p_v2[:, i, 1], last=True).then_inc(v_full, 1)
                if front:
                    pe.wait_ge(taken, 6 * k + 1)
                    pe.wait_ge(s_ready, k + 1)
                    scalars(w1_sb, lambda j: j, p_xs[:, 0], first=True)
                    pe.wait_ge(xsT_ready, k + 1)
                    front_x(s, 4, 3)
                    pe.wait_ge(taken, 6 * k + 2)
                    scalars(w1_sb, lambda j: 2 + j, p_xs[:, 1])
                    front_x(s, 5, 4)
                if back:
                    if not front or isinstance(k, int):
                        pe.wait_ge(w_ready, 7)
                    pe.wait_ge(s_ready, k + 1)
                    pe.wait_ge(v_ready, k + 1)
                    pe.wait_ge(raw_ready, 2 * k)
                    messages(0)
                if front:
                    front_y(6, 0)
                    pe.wait_ge(taken, 6 * k + 3)
                    scalars(w2_sb, lambda j: j, p_d[:, 0])
                if back:
                    pe.wait_ge(eq_ready, k)
                    pe.wait_ge(raw_ready, 2 * k + 1)
                    pe.wait_ge(msg_ready, 2 * k)
                    merge(0, z)
                    messages(1)
                if front:
                    front_y(7, 1)
                    pe.wait_ge(taken, 6 * k + 4)
                    scalars(w2_sb, lambda j: j, p_d[:, 1])
                if back:
                    pe.wait_ge(raw_ready, 2 * k + 2)
                    pe.wait_ge(msg_ready, 2 * k + 1)
                    merge(1, z)

            edge_chunk(0, 0, back=False)
            edge_chunk(1, 1)
            with pe.Fori(0, (NC - 3) // 2) as m:
                edge_chunk(2 * m + 2, 2)
                edge_chunk(2 * m + 3, 3)
            edge_chunk(NC - 1, NC - 1)
            edge_chunk(NC, NC, front=False)

        @block.scalar
        def _(act):
            def node_sqrt(g):
                act.wait_ge(mv_ready, g + 1)
                nc.scalar.activation(std[:], mv[:, :, 1], ACT.Sqrt, bias=eps_ap[:]).then_inc(std_ready, 1)

            def node_norm(g, j, half):
                s = j % 2
                act.wait_ge(norm_ready, g + 1)
                for t in range(4 * half, 4 * half + 4):
                    at = 224 * (t % 2)
                    last = nc.scalar.activation(hn[:, s, t // 2, at:at + D], x_sb[:, j % XS, t], ACT.Relu,
                                                bias=nbias[:, s, t:t + 1], scale=rstd[:, s, t:t + 1])
                last.then_inc(h_ready, 1)

            def node_evac(n, half):
                act.wait_ge(hT_full, n + 1)
                nc.scalar.activation(hT_a[:, half], bank[half][:], ACT.Copy)
                nc.scalar.activation(hT_b[:, half], bank[2 + half][:, 0:256], ACT.Copy).then_inc(hT_ready, 1)

            def node_group(g, j, norm_next=True, sqrt_next=True):
                node_norm(g, j, 1)
                node_evac(2 * g, 0)
                if norm_next:
                    node_norm(g + 1, j + 1, 0)
                node_evac(2 * g + 1, 1)
                if sqrt_next:
                    node_sqrt(g + 2)

            act.wait_ge(prep, 1)
            node_sqrt(0)
            node_norm(0, 0, 0)
            node_sqrt(1)
            node_group(0, 0)
            act.wait_ge(w_in2, 16 * N_W2)
            nc.scalar.activation(w1_sb[:], w1_raw[:], ACT.Copy, scale=float(C_S1)).then_inc(w_ready, 1)
            nc.scalar.activation(w2_sb[:], w2_raw[:], ACT.Copy, scale=float(C_S2)).then_inc(w_ready, 1)
            nc.scalar.activation(w3_sb[:], w3_raw[:], ACT.Copy, scale=float(C_V1)).then_inc(w_ready, 1)
            nc.scalar.activation(w4_sb[:], w4_raw[:], ACT.Copy, scale=float(C_V2)).then_inc(w_ready, 1)
            with act.Fori(0, (NG - 5) // 4) as q:
                for j in range(1, 5):
                    node_group(4 * q + j, j)
            for g in range(NG - 4, NG - 1):
                node_group(g, g, sqrt_next=g + 2 < NG)

            def edge_sqrt(c):
                act.wait_ge(g_mv, c + 1)
                nc.scalar.activation(e_std[:], e_mv[:, :, 1], ACT.Sqrt, bias=eps_ap[:]).then_inc(g_std, 1)

            def edge_norm(c, j, tiles, free=True):
                s = j % 2
                if tiles[0] == 0:
                    act.wait_ge(g_norm, c + 1)
                    if free:
                        act.wait_ge(front_full, 8 * c - 10)
                for t in tiles:
                    norm = dict(bias=e_nbias[:, s, t:t + 1], scale=e_rstd[:, s, t:t + 1])
                    sc = xg[:, s, t, 0:MUL0].rearrange("p (n a) -> p n a", n=2)
                    vc = xg[:, s, t, MUL0:D].rearrange("p (a i) -> p i a", i=3)
                    nc.scalar.activation(hg[:, s, t, 0:2], sc.unsqueeze(2).broadcast_to([P, 2, 4, 32]), ACT.Relu, **norm)
                    last = nc.scalar.activation(hg[:, s, t, 2:5], vc.unsqueeze(2).broadcast_to([P, 3, 4, 32]), ACT.Relu, **norm)
                if t == TPC - 1:
                    last.then_inc(g_h, 1)

            def raw_out(k, half):
                act.wait_ge(raw_full, 2 * k - 1 + half)
                nc.scalar.activation(raw_msg[:, 2 * half:2 * half + 2],
                                     bank[6][:, 0:2 * D].rearrange("p (t d) -> p t d", t=2),
                                     ACT.Copy).then_inc(raw_ready, 1)

            def msg_out(k, z, half):
                act.wait_ge(msg_full, 2 * k - 1 + half)
                if half == 0:
                    act.wait_ge(msg_free, k)
                    act.wait_ge(row_ready, k)
                    nc.scalar.activation(row_i[:, z], row_f[:, z], ACT.Copy)
                nc.scalar.activation(
                    msg[:, z, 2 * half:2 * half + 2], bank[7][:, 0:2 * D].rearrange("p (t d) -> p t d", t=2),
                    ACT.Copy).then_inc(msg_ready, 1)

            def edge_chunk(k, j, front=True, back=True, ahead=True):
                s, z = j % 2, (j + 1) % 2
                if front:
                    act.wait_ge(front_full, 8 * k + 1)
                    nc.scalar.activation(xsT[:], bank[0][0:MUL0, :], ACT.Copy).then_inc(xsT_ready, 1)
                if not back:
                    act.wait_ge(wc_mm, 3)
                    nc.scalar.activation(wc_s[0:MUL0], bank[6][0:MUL0, 0:D], ACT.Copy).then_inc(w_ready, 1)
                    nc.scalar.activation(wc_s[MUL0:P], bank[6][MUL0:P, 0:D], ACT.Copy).then_inc(w_ready, 1)
                    nc.scalar.activation(wc_v[:], bank[7][0:3 * MUL1 + 1, 0:D], ACT.Copy).then_inc(w_ready, 1)
                if back:
                    act.wait_ge(s_full, k)
                    nc.scalar.activation(tp_s[:], bank[4][:], ACT.Copy).then_inc(s_ready, 1)
                if ahead:
                    edge_sqrt(k + 1)
                if back:
                    act.wait_ge(v_full, k)
                    nc.scalar.activation(tp_v[0:3 * MUL1], bank[5][0:3 * MUL1, :], ACT.Copy).then_inc(v_ready, 1)
                if ahead:
                    edge_norm(k + 1, j + 1, [0], free=back)
                if front:
                    act.wait_ge(front_full, 8 * k + 6)
                    if back:
                        act.wait_ge(pool_d, k)
                    nc.scalar.activation(xv2[:], bank[1][:], ACT.Copy).then_inc(xv2_ready, 1)
                if ahead:
                    edge_norm(k + 1, j + 1, [1], free=back)
                if back:
                    raw_out(k, 0)
                if ahead:
                    edge_norm(k + 1, j + 1, [2, 3], free=back)
                if back:
                    msg_out(k, z, 0)
                    raw_out(k, 1)
                    msg_out(k, z, 1)

            act.sem_inc(s_ready, 1)
            act.sem_inc(v_ready, 1)
            act.sem_inc(raw_ready, 2)
            act.sem_inc(msg_ready, 2)
            edge_sqrt(0)
            node_group(NG - 1, NG - 1, norm_next=False, sqrt_next=False)
            edge_norm(0, 0, range(TPC), free=False)
            edge_chunk(0, 0, back=False)
            with act.Fori(0, (NC - 3) // 2) as m:
                edge_chunk(2 * m + 1, 1)
                edge_chunk(2 * m + 2, 2)
            edge_chunk(NC - 2, NC - 2)
            edge_chunk(NC - 1, NC - 1, ahead=False)
            edge_chunk(NC, NC, front=False, ahead=False)

        @block.vector
        def _(dve):
            nc.vector.memset(eps_ap[:], EPS)
            nc.vector.memset(tp_v[3 * MUL1:3 * MUL1 + 1, :], 1.0)
            nc.vector.memset(zero_rows[:], 0.0)
            pads = hn[:, :, :, D:D + 64].rearrange("p s n (a b) -> p (s n) a b", a=2)
            nc.vector.memset(pads[:, :, :, 1:32], 0.0)
            nc.vector.memset(pads[:, :, :, 0:1], 1.0).then_inc(prep, 1)
            def add_identity():
                dve.wait_ge(w_in, 16 * N_W)
                for o, one in ((wut_a[:, 0, 0:P], ident[:]), (wut_a[:, 1, D - P:D], ident[:]),
                               (wut_b[0:D - P, P:D], ident[0:D - P, 0:D - P]),
                               (wut_b[96:P, 0:32], ident[96:P, 96:P])):
                    last = nc.vector.tensor_tensor(o, o, one, ALU.add)
                last.then_inc(wut_ready, 2)

            def node_stats(g, j, arrived):
                s = j % 2
                dve.wait_ge(x_in[j % XS], arrived)
                for t in range(RPP):
                    last = nc.vector.bn_stats(bst[:, t], x_sb[:, j % XS, t])
                last.then_inc(stats_done, 1)
                dve.wait_ge(stats_done, g + 1)
                dve.sem_inc(passed_dve, 1)
                for t in range(RPP):
                    last = nc.vector.bn_aggr(mv[:, t], bst[:, t])
                last.then_inc(mv_ready, 1)

            def node_newton(g, j):
                newton(dve, nc.vector, mv[:, :, 1], mv[:, :, 0], j % 2, std, node_ln, std_ready, g + 1,
                       rstd_step, 4 * g, norm_ready)

            def node_add(g, j, half, y_free=None):
                s = j % 2
                if y_free is not None and half == 0:
                    dve.wait_ge(y_out[s], y_free)
                for b in range(2 * half, 2 * half + 2):
                    dve.wait_ge(out_full, 4 * g + b + 1)
                    r0_, r1_ = 4 * (b // 2) + b % 2, 4 * (b // 2) + 4
                    nc.vector.tensor_tensor(
                        y_sb[:, s, r0_:r1_:2], bank[4 + b][:, 0:2 * D].rearrange("p (t d) -> p t d", t=2),
                        x_sb[:, j % XS, r0_:r1_:2], ALU.add).then_inc(y_ready, 1)

            def node_group(g, j, arrived=None, y_free=None):
                if arrived is not None:
                    node_stats(g + 2, j + 2, arrived)
                node_add(g, j, 0, y_free)
                if arrived is not None:
                    node_newton(g + 2, j + 2)
                node_add(g, j, 1)

            def edge_stats(c, j, arrived):
                dve.wait_ge(xg_in[j % 2], arrived)
                for t in range(TPC):
                    last = nc.vector.bn_stats(e_bst[:, t], xg[:, j % 2, t])
                last.then_inc(g_stats, 1)
                dve.wait_ge(g_stats, c + 1)
                dve.sem_inc(passed_dve, 1)
                for t in range(TPC):
                    last = nc.vector.bn_aggr(e_mv[:, t], e_bst[:, t])
                last.then_inc(g_mv, 1)

            def edge_newton(c, j):
                newton(dve, nc.vector, e_mv[:, :, 1], e_mv[:, :, 0], j % 2, e_std, edge_ln, g_std, c + 1,
                       g_step, 4 * c, g_norm)

            node_stats(0, 0, 16)
            node_newton(0, 0)
            add_identity()
            node_stats(1, 1, 16)
            node_newton(1, 1)
            for g in range(2):
                node_group(g, g, 16)
            with dve.Fori(0, (NG - 5) // 4) as q:
                for j in range(2, 6):
                    node_group(4 * q + j, j, 16 * q + 16 * ((j + 2) // XS) + 16, 32 * q + 16 * (j // 2))
            for g in range(NG - 3, NG):
                last = g + 2 == NG - 1
                node_group(g, g, 16 * ((g + 2) // XS + 1) + 16 if last else None, 16 * (g // 2))
                if last:
                    edge_stats(0, 0, 64)
                if g == NG - 2:
                    edge_newton(0, 0)

            def times(o, pos, a):
                n = a.shape[1]
                return nc.vector.tensor_tensor(o, bank[pos % 4][:].unsqueeze(1).broadcast_to([P, n, CHUNK]), a, ALU.mult)

            def rows(k, s, arrived):
                dve.wait_ge(src_in[s], 2 * arrived)
                nc.vector.tensor_copy(src_f[:], src_sb[:, s]).then_inc(eq_step, 1)
                dve.wait_ge(eq_step, 4 * k + 1)
                for t in range(TPC):
                    nc.vector.scalar_tensor_tensor(
                        scrap[:, t], src_row[:, s, t * P:t * P + P], src_f[:, t:t + 1], before[:],
                        ALU.is_equal, ALU.mult, accum_out=n_before[:, t:t + 1])
                    last = nc.vector.tensor_scalar(equal[:, s, t], src_row[:, s, t * P:t * P + P], src_f[:, t:t + 1],
                                                   None, ALU.is_equal)
                last.then_inc(eq_ready, 1)
                nc.vector.tensor_scalar(to_spare[:], src_f[:], -1.0, spare_row[:], ALU.mult, ALU.add).then_inc(eq_step, 1)
                dve.wait_ge(eq_ready, k + 1)
                dve.wait_ge(eq_step, 4 * k + 2)
                nc.vector.scalar_tensor_tensor(shift[:], n_before[:], 0.5, to_spare[:], ALU.is_gt, ALU.mult).then_inc(eq_step, 2)
                dve.wait_ge(eq_step, 4 * k + 4)
                nc.vector.tensor_tensor(row_f[:, s], shift[:], src_f[:], ALU.add).then_inc(row_ready, 1)

            def edge_chunk(k, j, arrived, arrived2, prev=True, ahead=True):
                s = j % 2
                dve.wait_ge(attr_in[s], 4 * arrived)
                for h in range(2):
                    dve.wait_ge(front_full, 8 * k + 2 + h)
                    times(p_xs[:, h], 1 + h, attr[:, s, 0:2]).then_inc(taken, 1)
                if ahead:
                    edge_stats(k + 1, j + 1, arrived2)
                for i in range(2):
                    dve.wait_ge(front_full, 8 * k + 4 + i)
                    times(p_d[:, i], 3 + i, attr[:, s, 2 + 2 * i:4 + 2 * i])
                    if ahead and i == 0:
                        edge_newton(k + 1, j + 1)
                    if prev and i == 0:
                        dve.wait_ge(v_full, k)
                    times(p_v2[:, i], 3 + i, attr[:, s, 0:2]).then_inc(taken, 1)
                rows(k, s, arrived)
                for u in range(2):
                    dve.wait_ge(front_full, 8 * k + 7 + u)
                    times(p_y[:, u], 6 + u, attr[:, s, 2 + u:8:2]).then_inc(taken, 1)

            edge_chunk(0, 0, 16, 64, prev=False)
            with dve.Fori(0, (NC - 3) // 2) as m:
                edge_chunk(2 * m + 1, 1, 16 * m + 16, 64 * m + 128)
                edge_chunk(2 * m + 2, 2, 16 * m + 32, 64 * m + 128)
            n = NC // 2
            edge_chunk(NC - 2, NC - 2, 16 * n, 64 * n + 64)
            edge_chunk(NC - 1, NC - 1, 16 * n + 16, 0, ahead=False)

        @block.gpsimd
        def _(pool):
            pool.wait_ge(prep, 1)
            pool.sem_inc(msg_free, 2)
            pool.dma_start(out[N_NODES:OUT_ROWS, :], zero_rows[:]).then_inc(added, 16)

            def gather(s, t):
                nc.gpsimd.indirect_dma_start(
                    out=xg[:, s, t], out_offset=None, in_=x,
                    in_offset=bass.IndirectOffsetOnAxis(ap=dst_sb[:, s, t:t + 1], axis=0)).then_inc(xg_in[s], 16)

            def scatter(k2, s, t):
                if t == 0:
                    pool.wait_ge(msg_ready, 2 * k2 + 3)
                if t == 2:
                    pool.wait_ge(msg_ready, 2 * k2 + 4)
                pool.wait_ge(added, 64 * k2 + 16 * t + 16)
                pool.sem_inc(passed_pool, 1)
                nc.gpsimd.indirect_dma_start(
                    out=out, out_offset=bass.IndirectOffsetOnAxis(ap=row_i[:, s, t:t + 1], axis=0),
                    in_=msg[:, s, t], in_offset=None, compute_op=ALU.add).then_inc(added, 16)

            def product(o, s, n, done):
                nc.gpsimd.tensor_tensor(o, xv2[:].unsqueeze(1).broadcast_to([P, 2, CHUNK]),
                                        attr[:, s, n:n + 2], ALU.mult).then_inc(done, 1)

            def edge_chunk(k, j, arrived, arrived_attr, gathers=True, products=True, scatters=True):
                s = j % 2
                first = isinstance(k, int) and k == 0
                if scatters:
                    scatter(k - 2, s, 0)
                if gathers:
                    pool.wait_ge(dst_in[s], arrived)
                    pool.wait_ge(g_h, k + 1)
                    pool.sem_inc(passed_pool, 1)
                    gather(s, 0)
                    gather(s, 1)
                if scatters:
                    scatter(k - 2, s, 1)
                if gathers:
                    gather(s, 2)
                    gather(s, 3)
                if scatters:
                    scatter(k - 2, s, 2)
                if products:
                    pool.wait_ge(attr_in[s], arrived_attr)
                    pool.wait_ge(xv2_ready, k + 1)
                    product(p_d[:, 2], s, 6, pool_d1)
                if scatters:
                    scatter(k - 2, s, 3)
                if products:
                    if not first:
                        pool.wait_ge(v_full, k)
                    product(p_v2[:, 2], s, 0, pool_d)
                if scatters:
                    pool.wait_ge(added, 64 * k - 48)
                    pool.sem_inc(msg_free, 1)

            for s in range(2):
                pool.wait_ge(dst_in[s], 16)
                pool.sem_inc(passed_pool, 1)
                for t in range(TPC):
                    gather(s, t)
            edge_chunk(0, 0, 32, 64, scatters=False)
            edge_chunk(1, 1, 32, 64, scatters=False)
            pool.wait_ge(y_out[0], 16 * ((NG + 1) // 2) + 16)
            pool.wait_ge(y_out[1], 16 * (NG // 2))
            with pool.Fori(0, (NC - 5) // 2) as m:
                edge_chunk(2 * m + 2, 2, 16 * m + 48, 64 * m + 128)
                edge_chunk(2 * m + 3, 3, 16 * m + 48, 64 * m + 128)
            edge_chunk(NC - 3, NC - 3, 16 * (NC // 2) + 16, 64 * (NC // 2))
            edge_chunk(NC - 2, NC - 2, 0, 64 * (NC // 2), gathers=False)
            edge_chunk(NC - 1, NC - 1, 0, 64 * (NC // 2) + 64, gathers=False)
            edge_chunk(NC, NC, 0, 0, gathers=False, products=False)
            edge_chunk(NC + 1, NC + 1, 0, 0, gathers=False, products=False)


def kernel(**inputs):
    import numpy as _np
    import concourse.bacc as _bacc
    from concourse import mybir as _mybir
    from concourse.bass_utils import run_bass_kernel_spmd as _run

    get = lambda n: _np.ascontiguousarray(inputs[n])
    pad = E_PAD - N_EDGES
    dst = _np.concatenate([get("dst"), _np.zeros(pad, _np.int32)])
    src = _np.concatenate([get("src"), (N_NODES + _np.arange(N_EDGES, E_PAD) % P).astype(_np.int32)])
    attr = _np.concatenate([get("edge_attr_32"), _np.zeros((pad, DE), _np.float32)])
    order = _np.array([[MB * kind and (MB + 3 * b + kind - 1) or b for kind in range(4) for b in (4 * 0 + b4, 4 + b4)]
                       for b4 in range(4)])
    attr_t = attr[:, order.ravel()].reshape(NC, CHUNK, 4, 8).transpose(0, 2, 3, 1)
    hid = _np.concatenate([_np.arange(MUL0)] + [MUL0 + i + 3 * _np.arange(MUL1) for i in range(3)])
    w1, w2, w3, w4 = (get(f"L0_gnn_W{i}") for i in (1, 2, 3, 4))
    wm, wu = get("L0_gnn_Wm"), get("L0_gnn_Wu")
    eye = _np.eye(D, dtype=_np.float32)
    bu, none = get("L0_gnn_bu").reshape(1, D), _np.zeros((31, D), _np.float32)
    arrays = {
        "x": get("x"),
        "dst_cols": dst.reshape(NC, TPC, P).transpose(0, 2, 1),
        "src_cols": src.reshape(NC, TPC, P).transpose(0, 2, 1),
        "src_rows": src.reshape(NC, CHUNK),
        "attr_t": attr_t,
        "w1": w1.reshape(2, 32, 2, 4, MUL0).transpose(3, 1, 0, 2, 4).reshape(P, 4, MUL0),
        "w2": w2.reshape(32, 2, 4, MUL0).transpose(2, 0, 1, 3).reshape(P, 2, MUL0),
        "w3": w3.reshape(MUL0, 2, P),
        "w4": w4.reshape(32, 2, 4, MUL1).transpose(2, 0, 1, 3).reshape(P, 2, MUL1),
        "wm_bm_t": _np.concatenate([wm[hid], get("L0_gnn_bm").reshape(1, D)]).T,
        "wu_top_a": _np.stack([wu[:P], wu[D - P:D]], axis=1),
        "wu_top_b": _np.concatenate([wu[P:D], bu, none, bu, none, wu[:32]]),
        "wu_bot": wu[D:], "eye": eye[:P, :P],
        "delta": _np.tile(eye[:MUL1, :MUL1], (4, 1)),
        "earlier": _np.tril(_np.ones((P, P), _np.float32), -1),
        "spare": (N_NODES + _np.arange(P, dtype=_np.float32)).reshape(P, 1),
    }
    nc = _bacc.Bacc("TRN2", target_bir_lowering=False, num_devices=1)
    args = {}
    for name, a in arrays.items():
        arrays[name] = a = _np.ascontiguousarray(a)
        args[name] = nc.dram_tensor(name, a.shape, _mybir.dt.from_np(a.dtype), kind="ExternalInput").ap()
    out = nc.dram_tensor("out", (OUT_ROWS, D), _mybir.dt.float32, kind="ExternalOutput").ap()
    gnn_program(nc, *args.values(), out)
    got = _run(nc, [arrays], core_ids=[0]).results[0]["out"]
    return got[:N_NODES]
```

```python
import numpy as np
import concourse.bass as bass
from concourse import mybir
from contextlib import ExitStack

N_NODES, N_EDGES = 50000, 25000
D, DE = 160, 32
MUL0, MUL1, MB = 64, 32, 8
P = 128
EPS = 1e-5

RPP = 8
GROUP = P * RPP
NG = -(-N_NODES // GROUP)
TAIL_ROWS = N_NODES - (NG - 1) * GROUP
TAIL_P = TAIL_ROWS // RPP
TAIL_A = TAIL_P // 16 * 16
XS = 4

TPC = 4
CHUNK = TPC * P
NC = -(-N_EDGES // CHUNK)
E_PAD = NC * CHUNK
OUT_ROWS = N_NODES + P

C_S1 = 1.0 / np.sqrt(2.0) / np.sqrt(MUL0 * MB)
C_S2 = 1.0 / np.sqrt(2.0) / (np.sqrt(3.0) * np.sqrt(MUL1 * MB))
C_V1 = 1.0 / np.sqrt(2.0) / np.sqrt(MUL0 * MB)
C_V2 = 1.0 / np.sqrt(2.0) / np.sqrt(MUL1 * MB)


def gnn_program(nc, x, dst_cols, src_cols, src_rows, attr_t, w1, w2, w3, w4, wm_bm_t, wu_top_blocks,
                wu_bot, bu, eye, delta, places, spare, out):
    f32, i32 = mybir.dt.float32, mybir.dt.int32
    ALU, ACT = mybir.AluOpType, mybir.ActivationFunctionType
    ctx = ExitStack()

    def sb(name, shape, dt=f32):
        return ctx.enter_context(nc.sbuf_tensor(name, shape, dt))

    def sem(name):
        return ctx.enter_context(nc.semaphore(name))

    with ctx:
        bank = [ctx.enter_context(nc.psum_tensor(f"bank{i}", [P, 512], f32)) for i in range(8)]

        ident = sb("ident", [P, P])
        deltas = sb("deltas", [P, MUL1])
        place = sb("place", [P, TPC + 1])
        spare_row = sb("spare_row", [P, 1])
        w1_raw, w1_sb = sb("w1_raw", [P, 4, MUL0]), sb("w1_sb", [P, 4, MUL0])
        w2_raw, w2_sb = sb("w2_raw", [P, 2, MUL0]), sb("w2_sb", [P, 2, MUL0])
        w3_raw, w3_sb = sb("w3_raw", [P, 2, P]), sb("w3_sb", [P, 2, P])
        w4_raw, w4_sb = sb("w4_raw", [P, 2, MUL1]), sb("w4_sb", [P, 2, MUL1])
        wmT_a, wmT_b = sb("wmT_a", [P, D + 1]), sb("wmT_b", [D - P, D + 1])
        wub_a, wub_b = sb("wub_a", [P, D]), sb("wub_b", [D - P, D])
        wc_s, wc_v = sb("wc_s", [P, D]), sb("wc_v", [3 * MUL1 + 1, D])
        wut = sb("wut", [P, 8, D])
        bu_all = sb("bu_all", [P, D])
        eps_ap, one = sb("eps_ap", [P, 1]), sb("one", [P, 1])

        x_sb = sb("x_sb", [P, XS, RPP, D])
        y_sb = sb("y_sb", [P, 2, RPP, D])
        xb = sb("xb", [P, 2, RPP, D])
        hn = sb("hn", [P, 2, 2, 4 * D])
        hT = sb("hT", [P, 2, 5 * P])
        bst = sb("bst", [P, RPP, 6])
        mv = sb("mv", [P, RPP, 2])
        std = sb("std", [P, RPP])
        r0, r1, r2 = sb("r0", [P, RPP]), sb("r1", [P, RPP]), sb("r2", [P, RPP])
        rstd = sb("rstd", [P, 2, RPP])
        nbias = sb("nbias", [P, 2, RPP])
        node_ln = (r0, r1, r2, rstd, nbias)

        dst_sb = sb("dst_sb", [P, 2, TPC], i32)
        src_sb = sb("src_sb", [P, 2, TPC], i32)
        src_f = sb("src_f", [P, 2, TPC])
        src_row = sb("src_row", [P, 2, CHUNK], i32)
        attr = sb("attr", [P, 2, 8, CHUNK])
        xg = sb("xg", [P, 2, TPC, D])
        e_bst, e_mv, e_std = sb("e_bst", [P, TPC, 6]), sb("e_mv", [P, TPC, 2]), sb("e_std", [P, TPC])
        e_rstd, e_nbias = sb("e_rstd", [P, 2, TPC]), sb("e_nbias", [P, 2, TPC])
        edge_ln = (sb("e_r0", [P, TPC]), sb("e_r1", [P, TPC]), sb("e_r2", [P, TPC]), e_rstd, e_nbias)
        hg = sb("hg", [P, 2, TPC, 5, 4, 32])
        xsT = sb("xsT", [P, CHUNK])
        xv2 = sb("xv2", [P, CHUNK])
        p_xs = sb("p_xs", [P, 2, 2, CHUNK])
        p_v2 = sb("p_v2", [P, 3, 2, CHUNK])
        p_d = sb("p_d", [P, 3, 2, CHUNK])
        p_y = sb("p_y", [P, 2, 3, CHUNK])
        equal = sb("equal", [P, 2, TPC, P])
        to_spare, neg_src = sb("to_spare", [P, 2, TPC]), sb("neg_src", [P, TPC])
        apart = sb("apart", [P, TPC, P])
        shift = sb("shift", [P, 2, TPC])
        row_i = sb("row_i", [P, 2, TPC], i32)
        tp_s = sb("tp_s", [P, CHUNK])
        tp_v = sb("tp_v", [3 * MUL1 + 1, CHUNK])
        raw_msg = sb("raw_msg", [P, TPC, D + 1])
        msg = sb("msg", [P, 2, TPC, D + 1])
        zero_rows = sb("zero_rows", [P, D])

        w_in, w_in2 = sem("w_in"), sem("w_in2")
        wut_ready, bu_in, xb_ready = sem("wut_ready"), sem("bu_in"), sem("xb_ready")
        w_ready = sem("w_ready")
        wc_mm = sem("wc_mm")
        x_in = [sem(f"x_in{s}") for s in range(XS)]
        y_out = [sem(f"y_out{s}") for s in range(2)]
        stats_done, mv_ready, std_ready = sem("stats_done"), sem("mv_ready"), sem("std_ready")
        rstd_step, norm_ready = sem("rstd_step"), sem("norm_ready")
        h_ready, hT_full, hT_ready, out_full, y_ready = (
            sem(n) for n in ("h_ready", "hT_full", "hT_ready", "out_full", "y_ready"))
        prep = sem("prep")
        dst_in = [sem(f"dst_in{s}") for s in range(2)]
        src_in = [sem(f"src_in{s}") for s in range(2)]
        attr_in = [sem(f"attr_in{s}") for s in range(2)]
        xg_in = [sem(f"xg_in{s}") for s in range(2)]
        g_stats, g_mv, g_std, g_step, g_norm, g_h = (
            sem(n) for n in ("g_stats", "g_mv", "g_std", "g_step", "g_norm", "g_h"))
        front_full, taken = sem("front_full"), sem("taken")
        s_full, v_full, raw_full, msg_full = (sem(n) for n in ("s_full", "v_full", "raw_full", "msg_full"))
        xsT_ready, xv2_ready, s_ready, v_ready, raw_ready, msg_ready = (
            sem(n) for n in ("xsT_ready", "xv2_ready", "s_ready", "v_ready", "raw_ready", "msg_ready"))
        d_ready, pool_d1, pool_d = sem("d_ready"), sem("pool_d1"), sem("pool_d")
        eq_ready, eq_step, place_ready = sem("eq_ready"), sem("eq_step"), sem("place_ready")
        row_step, row_ready = sem("row_step"), sem("row_ready")
        spare_in = sem("spare_in")
        added = sem("added")
        msg_free = sem("msg_free")
        passed_sp = sem("passed_sp")
        passed_dve, passed_pool = sem("passed_dve"), sem("passed_pool")

        block = ctx.enter_context(nc.Block())

        def hg_block(s, t, n):
            return hg[:, s, t, n].rearrange("p b a -> p (b a)")

        def rows_of(dram, g):
            return dram[bass.ds(g * GROUP, GROUP), :].rearrange("(p r) d -> p r d", r=RPP)

        TB = (NG - 1) * GROUP

        def tail_of(dram, p0, p1):
            return dram[TB + p0 * RPP:TB + p1 * RPP, :].rearrange("(p r) d -> p r d", r=RPP)

        def newton(dve, var, mean, s, std, ln, std_sem, value, step, step0, done):
            r0, r1, r2, rstd, nbias = ln
            dve.wait_ge(std_sem, value)
            nc.vector.reciprocal(r0[:], std[:]).then_inc(step, 1)
            dve.wait_ge(step, step0 + 1)
            nc.vector.scalar_tensor_tensor(r1[:], var, EPS, r0[:], ALU.add, ALU.mult).then_inc(step, 1)
            dve.wait_ge(step, step0 + 2)
            nc.vector.scalar_tensor_tensor(r2[:], r1[:], -0.5, r0[:], ALU.mult, ALU.mult).then_inc(step, 1)
            dve.wait_ge(step, step0 + 3)
            nc.vector.scalar_tensor_tensor(rstd[:, s], r2[:], 1.5, r0[:], ALU.add, ALU.mult).then_inc(step, 1)
            dve.wait_ge(step, step0 + 4)
            nc.vector.scalar_tensor_tensor(nbias[:, s], mean, -1.0, rstd[:, s],
                                           ALU.mult, ALU.mult).then_inc(done, 1)

        N_W, N_W2 = 2, 11

        @block.sync
        def _(sp):
            node_loads = [(ident[:], eye), (wut[:], wu_top_blocks)]
            edge_loads = [
                (deltas[:], delta), (place[:], places), (spare_row[:], spare),
                (w1_raw[:], w1), (w2_raw[:], w2), (w3_raw[:], w3), (w4_raw[:], w4),
                (wmT_a[:], wm_bm_t[0:P, :]), (wmT_b[:], wm_bm_t[P:D, :]),
                (wub_a[:], wu_bot[0:P, :]), (wub_b[:], wu_bot[P:D, :]),
            ]
            assert len(node_loads) == N_W and len(edge_loads) == N_W2
            sp.dma_start(x_sb[:, 0], rows_of(x, 0)).then_inc(x_in[0], 16)
            sp.dma_start(bu_all[:], bu.partition_broadcast(P)).then_inc(bu_in, 16)
            for dst, src in node_loads:
                sp.dma_start(dst, src).then_inc(w_in, 16)
            for g in range(1, XS):
                sp.dma_start(x_sb[:, g], rows_of(x, g)).then_inc(x_in[g], 16)
            for dst, src in edge_loads:
                sp.dma_start(dst, src).then_inc(w_in2, 16)

            def edge_load(c, j, gathered=None, reused=True):
                s, z = j % 2, (j + 1) % 2
                if gathered is not None:
                    sp.wait_ge(xg_in[z], gathered)
                    sp.dma_start(dst_sb[:, z], dst_cols[c + 1]).then_inc(dst_in[z], 16)
                if reused:
                    sp.wait_ge(eq_ready, c - 1)
                sp.dma_start(src_sb[:, s], src_cols[c]).then_inc(src_in[s], 16)
                sp.dma_start(src_row[:, s], src_rows[c].partition_broadcast(P)).then_inc(src_in[s], 16)
                if reused:
                    sp.wait_ge(taken, 6 * (c - 1))
                    sp.wait_ge(pool_d, c - 1)
                for b in range(4):
                    if reused:
                        sp.wait_ge(*((taken, 6 * c - 5), (g_norm, c + 1), (d_ready, 2 * c - 1), (d_ready, 2 * c))[b])
                    sp.dma_start(attr[32 * b:32 * b + 32, s], attr_t[c, b].partition_broadcast(32)).then_inc(attr_in[s], 16)

            for c in range(2):
                sp.dma_start(dst_sb[:, c], dst_cols[c]).then_inc(dst_in[c], 16)
            edge_load(0, 0, reused=False)

            def store(g, j):
                sp.wait_ge(y_ready, (g + 1) * 4)
                sp.dma_start(rows_of(out, g), y_sb[:, j % 2]).then_inc(y_out[j % 2], 16)

            def load(g, j):
                sp.wait_ge(h_ready, 2 * (g - XS) + 2)
                sp.sem_inc(passed_sp, 1)
                sp.wait_ge(xb_ready, g - XS + 1)
                sp.dma_start(x_sb[:, j % XS], rows_of(x, g)).then_inc(x_in[j % XS], 16)

            with sp.Fori(0, (NG - 5) // XS) as q:
                for j in range(XS):
                    load(q * XS + j + XS, j)
                    store(q * XS + j, j)
            for g in range(NG - 5, NG - 1):
                if g + XS == NG - 1:
                    sp.wait_ge(h_ready, 2 * g + 2)
                    sp.wait_ge(xb_ready, g + 1)
                    sp.dma_start(x_sb[0:TAIL_A, g % XS], tail_of(x, 0, TAIL_A)).then_inc(x_in[g % XS], 16)
                    sp.dma_start(x_sb[TAIL_A:TAIL_P, g % XS], tail_of(x, TAIL_A, TAIL_P)).then_inc(x_in[g % XS], 16)
                store(g, g)
            sp.wait_ge(y_ready, NG * 4)
            s = (NG - 1) % 2
            sp.dma_start(tail_of(out, 0, TAIL_A), y_sb[0:TAIL_A, s]).then_inc(y_out[s], 16)
            sp.dma_start(tail_of(out, TAIL_A, TAIL_P), y_sb[TAIL_A:TAIL_P, s]).then_inc(y_out[s], 16)

            edge_load(1, 1, 64, reused=False)
            with sp.Fori(0, (NC - 3) // 2) as m:
                edge_load(2 * m + 2, 2, 64 * m + 64)
                edge_load(2 * m + 3, 3, 64 * m + 128)
            edge_load(NC - 1, NC - 1)
            sp.wait_ge(added, 16 * (1 + TPC * NC))

        @block.tensor
        def _(pe):
            pe.wait_ge(w_in, 16 * N_W)

            def transpose_half(n, s, half):
                pe.wait_ge(h_ready, n + 1)
                for b in range(5):
                    o = bank[half][:, b * P:b * P + P] if b < 4 else bank[2 + half][:, 0:P]
                    last = nc.tensor.transpose(o, hn[:, s, half, b * P:b * P + P], ident[:])
                last.then_inc(hT_full, 1)

            def update_half(n, half, first=False):
                pe.wait_ge(hT_ready, n + 1)
                for t in range(2):
                    if not first:
                        pe.wait_ge(y_ready, 2 * n + t - 3)
                    o = bank[4 + 2 * half + t]
                    for pair in range(2):
                        r = 2 * pair + t
                        for u in range(2):
                            last = nc.tensor.matmul(
                                o[:, pair * D:pair * D + D], hT[:, half, (r + u) * P:(r + u) * P + P], wut[:, 2 * r + u],
                                start=(pair == 0 and u == 0), stop=(pair == 1 and u == 1), skip_group_check=True)
                    last.then_inc(out_full, 1)

            def node_group(g, j):
                transpose_half(2 * g, j % 2, 0)
                update_half(2 * g - 1, 1)
                transpose_half(2 * g + 1, j % 2, 1)
                update_half(2 * g, 0)

            transpose_half(0, 0, 0)
            transpose_half(1, 0, 1)
            pe.wait_ge(wut_ready, 1)
            update_half(0, 0, first=True)
            transpose_half(2, 1, 0)
            update_half(1, 1, first=True)
            transpose_half(3, 1, 1)
            update_half(2, 0)
            with pe.Fori(0, (NG - 3) // 2) as q:
                node_group(2 * q + 2, 2)
                node_group(2 * q + 3, 3)
            node_group(NG - 1, NG - 1)
            update_half(2 * NG - 1, 1)

            def front_x(s, pos, n):
                for t in range(TPC):
                    last = nc.tensor.transpose(bank[pos][:, t * P:t * P + P], hg_block(s, t, n), ident[:])
                last.then_inc(front_full, 1)

            def front_y(pos, j):
                nc.tensor.matmul(bank[pos][:], w3_sb[:, j, :], xsT[:], start=True, stop=True).then_inc(front_full, 1)

            def scalars(w, n, p, first=False, last=False):
                for j in range(2):
                    mm = nc.tensor.matmul(bank[4][MUL0 * j:MUL0 * j + MUL0, :], w[:, n(j), :], p[:, j, :],
                                          start=first, stop=last)
                if last:
                    mm.then_inc(s_full, 1)

            def vectors(w, p, first=False, last=False):
                for i in range(3):
                    mm = nc.tensor.matmul(bank[5][MUL1 * i:MUL1 * i + MUL1, :], w, p(i), start=first, stop=last)
                return mm

            def messages(half):
                for u in range(2):
                    t = 2 * half + u
                    nc.tensor.matmul(bank[6][:, u * D:u * D + D], tp_s[:, t * P:t * P + P], wc_s[:],
                                     start=(u == 0), stop=False, skip_group_check=True)
                    mm = nc.tensor.matmul(bank[6][:, u * D:u * D + D], tp_v[:, t * P:t * P + P], wc_v[:],
                                          start=False, stop=(u == 1), skip_group_check=True)
                mm.then_inc(raw_full, 1)

            def merge(half, z):
                for u in range(2):
                    t = 2 * half + u
                    mm = nc.tensor.matmul(bank[7][:, u * (D + 1):(u + 1) * (D + 1)], equal[:, z, t, :], raw_msg[:, t, :],
                                          start=(u == 0), stop=(u == 1), skip_group_check=True)
                mm.then_inc(msg_full, 1)

            def combine_weights():
                for rows, o, p0 in ((slice(0, MUL0), bank[6], 0), (slice(0, MUL0), bank[6], MUL0),
                                    (slice(MUL0, D + 1), bank[7], 0)):
                    p1 = p0 + rows.stop - rows.start
                    nc.tensor.matmul(o[p0:p1, 0:D], wmT_a[:, rows], wub_a[:], start=True, stop=False)
                    nc.tensor.matmul(o[p0:p1, 0:D], wmT_b[:, rows], wub_b[:], start=False, stop=True).then_inc(wc_mm, 1)

            def edge_chunk(k, j, front=True, back=True):
                s, z = j % 2, (j + 1) % 2
                if front:
                    pe.wait_ge(g_h, k + 1)
                    if back:
                        pe.wait_ge(xv2_ready, k)
                    front_x(s, 0, 0)
                    if back:
                        pe.wait_ge(taken, 6 * k - 1)
                    front_x(s, 1, 1)
                    front_x(s, 3, 3)
                    if back:
                        pe.wait_ge(taken, 6 * k)
                    front_x(s, 2, 2)
                if back:
                    pe.wait_ge(pool_d1, k)
                    scalars(w2_sb, lambda j: j, p_d[:, 2], last=True)
                if not back:
                    pe.wait_ge(y_ready, 4 * NG)
                    pe.wait_ge(w_ready, 4)
                if back:
                    pe.wait_ge(taken, 6 * k)
                    pe.wait_ge(pool_d, k)
                    pe.wait_ge(v_ready, k)
                    vectors(deltas[:], lambda i: p_y[:, 0, i], first=True)
                    vectors(deltas[:], lambda i: p_y[:, 1, i])
                    vectors(w4_sb[:, 0, :], lambda i: p_v2[:, i, 0])
                    vectors(w4_sb[:, 1, :], lambda i: p_v2[:, i, 1], last=True).then_inc(v_full, 1)
                if front:
                    pe.wait_ge(taken, 6 * k + 1)
                    pe.wait_ge(s_ready, k + 1)
                    scalars(w1_sb, lambda j: j, p_xs[:, 0], first=True)
                    pe.wait_ge(taken, 6 * k + 2)
                    scalars(w1_sb, lambda j: 2 + j, p_xs[:, 1])
                    pe.wait_ge(xsT_ready, 2 * k + 1)
                    front_x(s, 0, 4)
                if back:
                    if not front or isinstance(k, int):
                        pe.wait_ge(place_ready, 1)
                        pe.wait_ge(w_ready, 7)
                    pe.wait_ge(s_ready, k + 1)
                    pe.wait_ge(v_ready, k + 1)
                    pe.wait_ge(raw_ready, 2 * k)
                    messages(0)
                if front:
                    pe.wait_ge(xsT_ready, 2 * k + 2)
                    front_y(1, 0)
                if back:
                    pe.wait_ge(eq_ready, k)
                    pe.wait_ge(raw_ready, 2 * k + 1)
                    pe.wait_ge(msg_ready, 2 * k)
                    merge(0, z)
                    messages(1)
                if not back:
                    combine_weights()
                if front:
                    pe.wait_ge(taken, 6 * k + 4)
                    front_y(2, 1)
                    pe.wait_ge(d_ready, 2 * k + 2)
                    scalars(w2_sb, lambda j: j, p_d[:, 0])
                if back:
                    pe.wait_ge(raw_ready, 2 * k + 2)
                    pe.wait_ge(msg_ready, 2 * k + 1)
                    merge(1, z)

            edge_chunk(0, 0, back=False)
            edge_chunk(1, 1)
            with pe.Fori(0, (NC - 3) // 2) as m:
                edge_chunk(2 * m + 2, 2)
                edge_chunk(2 * m + 3, 3)
            edge_chunk(NC - 1, NC - 1)
            edge_chunk(NC, NC, front=False)

        @block.scalar
        def _(act):
            def node_sqrt(g):
                act.wait_ge(mv_ready, g + 1)
                nc.scalar.activation(std[:], mv[:, :, 1], ACT.Sqrt, bias=eps_ap[:]).then_inc(std_ready, 1)

            def node_norm(g, j, half):
                s = j % 2
                act.wait_ge(norm_ready, g + 1)
                for t in range(4 * half, 4 * half + 4):
                    at = D * (t % 4)
                    last = nc.scalar.activation(hn[:, s, half, at:at + D], x_sb[:, j % XS, t], ACT.Relu,
                                                bias=nbias[:, s, t:t + 1], scale=rstd[:, s, t:t + 1])
                last.then_inc(h_ready, 1)

            def node_evac(n, half):
                act.wait_ge(hT_full, n + 1)
                nc.scalar.activation(hT[:, half, 0:4 * P], bank[half][:], ACT.Copy)
                nc.scalar.activation(hT[:, half, 4 * P:5 * P], bank[2 + half][:, 0:P], ACT.Copy).then_inc(hT_ready, 1)

            def node_group(g, j, norm_next=True, sqrt_next=True):
                node_norm(g, j, 1)
                node_evac(2 * g, 0)
                if norm_next:
                    node_norm(g + 1, j + 1, 0)
                node_evac(2 * g + 1, 1)
                if sqrt_next:
                    node_sqrt(g + 2)

            act.wait_ge(prep, 1)
            nc.scalar.activation(e_std[:, 0:1], eps_ap[:], ACT.Sqrt)
            node_sqrt(0)
            node_norm(0, 0, 0)
            node_sqrt(1)
            node_group(0, 0)
            act.wait_ge(w_in2, 16 * N_W2)
            nc.scalar.activation(w1_sb[:], w1_raw[:], ACT.Copy, scale=float(C_S1)).then_inc(w_ready, 1)
            nc.scalar.activation(w2_sb[:], w2_raw[:], ACT.Copy, scale=float(C_S2)).then_inc(w_ready, 1)
            nc.scalar.activation(w3_sb[:], w3_raw[:], ACT.Copy, scale=float(C_V1)).then_inc(w_ready, 1)
            nc.scalar.activation(w4_sb[:], w4_raw[:], ACT.Copy, scale=float(C_V2)).then_inc(w_ready, 1)
            with act.Fori(0, (NG - 5) // 4) as q:
                for j in range(1, 5):
                    node_group(4 * q + j, j)
            for g in range(NG - 4, NG - 1):
                node_group(g, g, sqrt_next=g + 2 < NG)

            def edge_sqrt(c):
                act.wait_ge(g_mv, c + 1)
                nc.scalar.activation(e_std[:], e_mv[:, :, 1], ACT.Sqrt, bias=eps_ap[:]).then_inc(g_std, 1)

            def edge_norm(c, j, tiles, free=True):
                s = j % 2
                if tiles[0] == 0:
                    act.wait_ge(g_norm, c + 1)
                    if free:
                        act.wait_ge(front_full, 7 * c - 9)
                for t in tiles:
                    norm = dict(bias=e_nbias[:, s, t:t + 1], scale=e_rstd[:, s, t:t + 1])
                    sc = xg[:, s, t, 0:MUL0].rearrange("p (n a) -> p n a", n=2)
                    vc = xg[:, s, t, MUL0:D].rearrange("p (a i) -> p i a", i=3)
                    nc.scalar.activation(hg[:, s, t, 0:2], sc.unsqueeze(2).broadcast_to([P, 2, 4, 32]), ACT.Relu, **norm)
                    last = nc.scalar.activation(hg[:, s, t, 2:5], vc.unsqueeze(2).broadcast_to([P, 3, 4, 32]), ACT.Relu, **norm)
                if t == TPC - 1:
                    last.then_inc(g_h, 1)

            def equality(k, j, arrived):
                s = j % 2
                act.wait_ge(src_in[s], 2 * arrived)
                if not (isinstance(k, int) and k < 2):
                    act.wait_ge(row_ready, k - 1)
                nc.scalar.activation(src_f[:, s], src_sb[:, s], ACT.Copy)
                nc.scalar.activation(to_spare[:, s], src_sb[:, s], ACT.Identity, scale=-1.0, bias=spare_row[:])
                nc.scalar.activation(neg_src[:], src_sb[:, s], ACT.Copy, scale=-1.0).then_inc(eq_step, 1)
                act.wait_ge(eq_step, 2 * k + 1)
                for t in range(TPC):
                    last = nc.scalar.activation(apart[:, t], src_row[:, s, t * P:t * P + P], ACT.Square, bias=neg_src[:, t:t + 1])
                last.then_inc(eq_step, 1)

            def equality_end(k, j):
                s = j % 2
                act.wait_ge(eq_step, 2 * k + 2)
                nc.scalar.activation(equal[:, s], apart[:], ACT.Relu, scale=-1.0, bias=one[:]).then_inc(eq_ready, 1)

            def raw_out(k, half):
                act.wait_ge(raw_full, 2 * k - 1 + half)
                nc.scalar.activation(raw_msg[:, 2 * half:2 * half + 2, 0:D],
                                     bank[6][:, 0:2 * D].rearrange("p (t d) -> p t d", t=2),
                                     ACT.Copy).then_inc(raw_ready, 1)

            def msg_out(k, z, half):
                act.wait_ge(msg_full, 2 * k - 1 + half)
                if half == 0:
                    act.wait_ge(msg_free, k)
                nc.scalar.activation(
                    msg[:, z, 2 * half:2 * half + 2],
                    bank[7][:, 0:2 * (D + 1)].rearrange("p (t d) -> p t d", t=2),
                    ACT.Copy).then_inc(msg_ready, 1)

            def edge_chunk(k, j, arrived, front=True, back=True, ahead=True):
                s, z = j % 2, (j + 1) % 2
                if front:
                    for h in range(2):
                        act.wait_ge(front_full, 7 * k + 1 + h)
                        nc.scalar.activation(xsT[32 * h:32 * h + 32], bank[h][32 * h:32 * h + 32, :],
                                             ACT.Copy).then_inc(xsT_ready, 1)
                if back:
                    act.wait_ge(s_full, k)
                    nc.scalar.activation(tp_s[:], bank[4][:], ACT.Copy).then_inc(s_ready, 1)
                if front:
                    equality(k, j, arrived)
                if ahead:
                    edge_sqrt(k + 1)
                if front:
                    equality_end(k, j)
                if back:
                    act.wait_ge(v_full, k)
                    nc.scalar.activation(tp_v[0:3 * MUL1], bank[5][0:3 * MUL1, :], ACT.Copy).then_inc(v_ready, 1)
                if ahead:
                    edge_norm(k + 1, j + 1, [0], free=back)
                if front:
                    act.wait_ge(front_full, 7 * k + 5)
                    if back:
                        act.wait_ge(pool_d, k)
                    nc.scalar.activation(xv2[:], bank[0][:], ACT.Copy).then_inc(xv2_ready, 1)
                if back:
                    raw_out(k, 0)
                if ahead:
                    edge_norm(k + 1, j + 1, [1, 2], free=back)
                if back:
                    msg_out(k, z, 0)
                    raw_out(k, 1)
                if ahead:
                    edge_norm(k + 1, j + 1, [3], free=back)
                if back:
                    msg_out(k, z, 1)
                else:
                    act.wait_ge(wc_mm, 3)
                    nc.scalar.activation(wc_s[0:MUL0], bank[6][0:MUL0, 0:D], ACT.Copy).then_inc(w_ready, 1)
                    nc.scalar.activation(wc_s[MUL0:P], bank[6][MUL0:P, 0:D], ACT.Copy).then_inc(w_ready, 1)
                    nc.scalar.activation(wc_v[:], bank[7][0:3 * MUL1 + 1, 0:D], ACT.Copy).then_inc(w_ready, 1)

            act.sem_inc(s_ready, 1)
            act.sem_inc(v_ready, 1)
            act.sem_inc(raw_ready, 2)
            act.sem_inc(msg_ready, 2)
            edge_sqrt(0)
            node_group(NG - 1, NG - 1, norm_next=False, sqrt_next=False)
            edge_norm(0, 0, range(TPC), free=False)
            edge_chunk(0, 0, 16, back=False)
            edge_chunk(1, 1, 16)
            with act.Fori(0, (NC - 5) // 2) as m:
                edge_chunk(2 * m + 2, 2, 16 * m + 32)
                edge_chunk(2 * m + 3, 3, 16 * m + 32)
            edge_chunk(NC - 3, NC - 3, 16 * (NC // 2))
            edge_chunk(NC - 2, NC - 2, 16 * (NC // 2))
            edge_chunk(NC - 1, NC - 1, 16 * (NC // 2) + 16, ahead=False)
            edge_chunk(NC, NC, 0, front=False, ahead=False)

        @block.vector
        def _(dve):
            nc.vector.memset(eps_ap[:], EPS)
            nc.vector.memset(one[:], 1.0)
            nc.vector.memset(tp_v[3 * MUL1:3 * MUL1 + 1, :], 1.0)
            nc.vector.memset(xsT[MUL0:P, :], 0.0)
            nc.vector.memset(zero_rows[:], 0.0).then_inc(prep, 1)

            def add_identity():
                dve.wait_ge(w_in, 16 * N_W)
                for r in range(4):
                    ranges = [(32 * r, P)] if r != 1 else [(32, 64), (64, P)]
                    for a, b in ranges:
                        nc.vector.tensor_tensor(wut[a:b, 2 * r, a - 32 * r:b - 32 * r], wut[a:b, 2 * r, a - 32 * r:b - 32 * r],
                                                ident[a:b, a:b], ALU.add)
                    b, c0 = 32 * r + 32, P - 32 * r
                    last = nc.vector.tensor_tensor(wut[0:b, 2 * r + 1, c0:c0 + b], wut[0:b, 2 * r + 1, c0:c0 + b],
                                                   ident[0:b, 0:b], ALU.add)
                last.then_inc(wut_ready, 1)

            def node_stats(g, j, arrived):
                s = j % 2
                dve.wait_ge(x_in[j % XS], arrived)
                for t in range(RPP):
                    last = nc.vector.bn_stats(bst[:, t], x_sb[:, j % XS, t])
                last.then_inc(stats_done, 1)
                dve.wait_ge(stats_done, g + 1)
                dve.sem_inc(passed_dve, 1)
                for t in range(RPP):
                    last = nc.vector.bn_aggr(mv[:, t], bst[:, t])
                last.then_inc(mv_ready, 1)

            def node_newton(g, j):
                newton(dve, mv[:, :, 1], mv[:, :, 0], j % 2, std, node_ln, std_ready, g + 1,
                       rstd_step, 4 * g, norm_ready)

            def node_add(g, j, half, y_free=None):
                s = j % 2
                if half == 0:
                    dve.wait_ge(xb_ready, g + 1)
                if y_free is not None and half == 0:
                    dve.wait_ge(y_out[s], y_free)
                for b in range(2 * half, 2 * half + 2):
                    dve.wait_ge(out_full, 4 * g + b + 1)
                    r0_, r1_ = 4 * (b // 2) + b % 2, 4 * (b // 2) + 4
                    nc.vector.tensor_tensor(
                        y_sb[:, s, r0_:r1_:2], bank[4 + b][:, 0:2 * D].rearrange("p (t d) -> p t d", t=2),
                        xb[:, s, r0_:r1_:2], ALU.add).then_inc(y_ready, 1)

            def node_group(g, j, arrived=None, y_free=None, newton_next=True):
                node_add(g, j, 0, y_free)
                if newton_next:
                    node_newton(g + 2, j + 2)
                if arrived is not None:
                    node_stats(g + 3, j + 3, arrived)
                node_add(g, j, 1)

            def edge_stats(c, j, arrived):
                dve.wait_ge(xg_in[j % 2], arrived)
                for t in range(TPC):
                    last = nc.vector.bn_stats(e_bst[:, t], xg[:, j % 2, t])
                last.then_inc(g_stats, 1)
                dve.wait_ge(g_stats, c + 1)
                dve.sem_inc(passed_dve, 1)
                for t in range(TPC):
                    last = nc.vector.bn_aggr(e_mv[:, t], e_bst[:, t])
                last.then_inc(g_mv, 1)

            def edge_newton(c, j):
                newton(dve, e_mv[:, :, 1], e_mv[:, :, 0], j % 2, e_std, edge_ln, g_std, c + 1,
                       g_step, 4 * c, g_norm)

            node_stats(0, 0, 16)
            node_newton(0, 0)
            node_stats(1, 1, 16)
            node_newton(1, 1)
            add_identity()
            node_stats(2, 2, 16)
            for g in range(2):
                node_group(g, g, 16 * ((g + 3) // XS + 1))
            with dve.Fori(0, (NG - 9) // 4) as q:
                for j in range(2, 6):
                    node_group(4 * q + j, j, 16 * q + 16 * ((j + 3) // XS) + 16, 32 * q + 16 * (j // 2))
            for g in range(NG - 7, NG):
                arrived = 16 * ((g + 3) // XS) + (32 if g + 3 == NG - 1 else 16)
                node_group(g, g, arrived if g + 3 < NG else None, 16 * (g // 2), newton_next=g + 2 < NG)
                if g == NG - 3:
                    edge_stats(0, 0, 64)
                if g == NG - 2:
                    edge_newton(0, 0)

            def times(o, pos, a):
                n = a.shape[1]
                return nc.vector.tensor_tensor(o, bank[pos][:].unsqueeze(1).broadcast_to([P, n, CHUNK]), a, ALU.mult)

            def rows(c, j, half=None, before=0):
                s, ts = j % 2, slice(0, TPC) if half is None else slice(2 * half, 2 * half + 2)
                dve.wait_ge(msg_ready, 2 * c + 3 + (1 if half is None else half))
                done = c + 1 if half is None else NC - 1 + before
                nc.vector.scalar_tensor_tensor(shift[:, s, ts], msg[:, s, ts, D], place[:, TPC:TPC + 1],
                                               to_spare[:, s, ts], ALU.is_gt, ALU.mult).then_inc(row_step, 1)
                dve.wait_ge(row_step, done)
                nc.vector.tensor_tensor(row_i[:, s, ts], shift[:, s, ts], src_f[:, s, ts], ALU.add).then_inc(row_ready, 1)

            def edge_chunk(k, j, arrived, arrived2, prev=True, ahead=True, last=False):
                s = j % 2
                if not (isinstance(k, int) and k < 2):
                    rows(k - 2, j)
                dve.wait_ge(attr_in[s], 4 * arrived)
                for h in range(2):
                    dve.wait_ge(xsT_ready, 2 * k + 1 + h)
                    times(p_xs[:, h], h, attr[:, s, 0:2]).then_inc(taken, 1)
                    if ahead and h == 0:
                        edge_stats(k + 1, j + 1, arrived2)
                if ahead:
                    edge_newton(k + 1, j + 1)
                for n, i in enumerate((1, 0)):
                    dve.wait_ge(front_full, 7 * k + 3 + n)
                    product = times(p_d[:, i], 2 + i, attr[:, s, 2 + 2 * i:4 + 2 * i])
                    if n == 1:
                        product.then_inc(d_ready, 1)
                    if prev and n == 0:
                        dve.wait_ge(v_full, k)
                    times(p_v2[:, i], 2 + i, attr[:, s, 0:2]).then_inc(taken, 1)
                dve.wait_ge(d_ready, 2 * k + 1)
                nc.vector.tensor_tensor(p_d[:, 0], p_d[:, 0], p_d[:, 1], ALU.add).then_inc(d_ready, 1)
                for u in range(2):
                    if last and u == 1:
                        rows(k - 1, j + 1, 0)
                    dve.wait_ge(front_full, 7 * k + 6 + u)
                    times(p_y[:, u], 1 + u, attr[:, s, 2 + u:8:2]).then_inc(taken, 1)

            dve.wait_ge(w_in2, 16 * N_W2)
            nc.vector.tensor_copy(raw_msg[:, :, D], place[:, 0:TPC]).then_inc(place_ready, 1)
            edge_chunk(0, 0, 16, 64, prev=False)
            edge_chunk(1, 1, 16, 128)
            with dve.Fori(0, (NC - 5) // 2) as m:
                edge_chunk(2 * m + 2, 2, 16 * m + 32, 64 * m + 128)
                edge_chunk(2 * m + 3, 3, 16 * m + 32, 64 * m + 192)
            n = NC // 2
            edge_chunk(NC - 3, NC - 3, 16 * n, 64 * n)
            edge_chunk(NC - 2, NC - 2, 16 * n, 64 * n + 64)
            edge_chunk(NC - 1, NC - 1, 16 * n + 16, 0, ahead=False, last=True)
            rows(NC - 2, NC - 2, 1, before=1)
            rows(NC - 1, NC - 1, 0, before=2)
            rows(NC - 1, NC - 1, 1, before=3)

        @block.gpsimd
        def _(pool):
            pool.wait_ge(prep, 1)
            pool.sem_inc(msg_free, 2)
            pool.dma_start(out[N_NODES:OUT_ROWS, :], zero_rows[:]).then_inc(added, 16)

            def gather(s, t):
                nc.gpsimd.indirect_dma_start(
                    out=xg[:, s, t], out_offset=None, in_=x,
                    in_offset=bass.IndirectOffsetOnAxis(ap=dst_sb[:, s, t:t + 1], axis=0)).then_inc(xg_in[s], 16)

            def scatter(k2, s, t):
                if isinstance(k2, int) and k2 >= NC - 2:
                    if t % 2 == 0:
                        pool.wait_ge(row_ready, NC - 1 + 2 * (k2 - (NC - 2)) + t // 2)
                elif t == 0:
                    pool.wait_ge(row_ready, k2 + 1)
                pool.wait_ge(added, 64 * k2 + 16 * t + 16)
                pool.sem_inc(passed_pool, 1)
                nc.gpsimd.indirect_dma_start(
                    out=out, out_offset=bass.IndirectOffsetOnAxis(ap=row_i[:, s, t:t + 1], axis=0),
                    in_=msg[:, s, t, 0:D], in_offset=None, compute_op=ALU.add).then_inc(added, 16)

            def product(o, s, n, done):
                nc.gpsimd.tensor_tensor(o, xv2[:].unsqueeze(1).broadcast_to([P, 2, CHUNK]),
                                        attr[:, s, n:n + 2], ALU.mult).then_inc(done, 1)

            def edge_chunk(k, j, arrived, arrived_attr, gathers=True, products=True, scatters=True):
                s = j % 2
                first = isinstance(k, int) and k == 0
                if scatters:
                    scatter(k - 2, s, 0)
                if gathers:
                    pool.wait_ge(dst_in[s], arrived)
                    pool.wait_ge(g_h, k + 1)
                    pool.sem_inc(passed_pool, 1)
                    gather(s, 0)
                    gather(s, 1)
                if scatters:
                    scatter(k - 2, s, 1)
                if gathers:
                    gather(s, 2)
                    gather(s, 3)
                if scatters:
                    scatter(k - 2, s, 2)
                if products:
                    pool.wait_ge(attr_in[s], arrived_attr)
                    pool.wait_ge(xv2_ready, k + 1)
                    product(p_d[:, 2], s, 6, pool_d1)
                if scatters:
                    scatter(k - 2, s, 3)
                if products:
                    if not first:
                        pool.wait_ge(v_full, k)
                    product(p_v2[:, 2], s, 0, pool_d)
                if scatters:
                    pool.wait_ge(added, 64 * k - 48)
                    pool.sem_inc(msg_free, 1)

            def add_bias(g, j, arrived, reused=True):
                pool.wait_ge(x_in[j % XS], arrived)
                if reused:
                    pool.wait_ge(y_ready, 4 * (g - 1))
                nc.gpsimd.tensor_tensor(xb[:, j % 2], x_sb[:, j % XS], bu_all[:].unsqueeze(1).broadcast_to([P, RPP, D]),
                                        ALU.add).then_inc(xb_ready, 1)

            pool.wait_ge(bu_in, 16)
            for g in range(2):
                add_bias(g, g, 16, reused=False)
            for s in range(2):
                pool.wait_ge(dst_in[s], 16)
                pool.sem_inc(passed_pool, 1)
                for t in range(TPC):
                    gather(s, t)
            with pool.Fori(0, (NG - 5) // 4) as q:
                for j in range(2, 6):
                    add_bias(4 * q + j, j, 16 * q + 16 * (j // XS) + 16)
            for g in range(NG - 3, NG):
                add_bias(g, g, 16 * (g // XS) + (32 if g == NG - 1 else 16))
            edge_chunk(0, 0, 32, 64, scatters=False)
            edge_chunk(1, 1, 32, 64, scatters=False)
            pool.wait_ge(y_out[0], 16 * ((NG + 1) // 2) + 16)
            pool.wait_ge(y_out[1], 16 * (NG // 2))
            with pool.Fori(0, (NC - 5) // 2) as m:
                edge_chunk(2 * m + 2, 2, 16 * m + 48, 64 * m + 128)
                edge_chunk(2 * m + 3, 3, 16 * m + 48, 64 * m + 128)
            edge_chunk(NC - 3, NC - 3, 16 * (NC // 2) + 16, 64 * (NC // 2))
            edge_chunk(NC - 2, NC - 2, 0, 64 * (NC // 2), gathers=False)
            edge_chunk(NC - 1, NC - 1, 0, 64 * (NC // 2) + 64, gathers=False)
            edge_chunk(NC, NC, 0, 0, gathers=False, products=False)
            edge_chunk(NC + 1, NC + 1, 0, 0, gathers=False, products=False)


def kernel(**inputs):
    import numpy as _np
    import concourse.bacc as _bacc
    from concourse import mybir as _mybir
    from concourse.bass_utils import run_bass_kernel_spmd as _run

    get = lambda n: _np.ascontiguousarray(inputs[n])
    pad = E_PAD - N_EDGES
    dst = _np.concatenate([get("dst"), _np.zeros(pad, _np.int32)])
    src = _np.concatenate([get("src"), (N_NODES + _np.arange(N_EDGES, E_PAD) % P).astype(_np.int32)])
    attr = _np.concatenate([get("edge_attr_32"), _np.zeros((pad, DE), _np.float32)])
    order = _np.array([[MB * kind and (MB + 3 * b + kind - 1) or b for kind in range(4) for b in (4 * 0 + b4, 4 + b4)]
                       for b4 in range(4)])
    attr_t = attr[:, order.ravel()].reshape(NC, CHUNK, 4, 8).transpose(0, 2, 3, 1)
    hid = _np.concatenate([_np.arange(MUL0)] + [MUL0 + i + 3 * _np.arange(MUL1) for i in range(3)])
    w1, w2, w3, w4 = (get(f"L0_gnn_W{i}") for i in (1, 2, 3, 4))
    wm, wu = get("L0_gnn_Wm"), get("L0_gnn_Wu")
    eye = _np.eye(D, dtype=_np.float32)
    zeros = _np.zeros((P, D), _np.float32)
    arrays = {
        "x": get("x"),
        "dst_cols": dst.reshape(NC, TPC, P).transpose(0, 2, 1),
        "src_cols": src.reshape(NC, TPC, P).transpose(0, 2, 1),
        "src_rows": src.reshape(NC, CHUNK),
        "attr_t": attr_t,
        "w1": w1.reshape(2, 32, 2, 4, MUL0).transpose(3, 1, 0, 2, 4).reshape(P, 4, MUL0),
        "w2": w2.reshape(32, 2, 4, MUL0).transpose(2, 0, 1, 3).reshape(P, 2, MUL0),
        "w3": _np.concatenate([w3.reshape(MUL0, 2, P), zeros[:MUL0, 0:P, None].transpose(0, 2, 1).repeat(2, axis=1)]),
        "w4": w4.reshape(32, 2, 4, MUL1).transpose(2, 0, 1, 3).reshape(P, 2, MUL1),
        "wm_bm_t": _np.concatenate([wm[hid], get("L0_gnn_bm").reshape(1, D)]).T,
        "wu_top_blocks": _np.stack([b for r in range(4) for b in (
            _np.concatenate([zeros[:32 * r], wu[:P - 32 * r]]),
            _np.concatenate([wu[P - 32 * r:D], zeros[:96 - 32 * r]]))], axis=1),
        "wu_bot": wu[D:], "bu": get("L0_gnn_bu").reshape(D), "eye": eye[:P, :P],
        "delta": _np.tile(eye[:MUL1, :MUL1], (4, 1)),
        "places": (2.0 ** (60 - _np.arange(P, dtype=_np.float64)).reshape(P, 1) * [[1] * TPC + [2.5]]).astype(_np.float32),
        "spare": (N_NODES + _np.arange(P, dtype=_np.float32)).reshape(P, 1),
    }
    nc = _bacc.Bacc("TRN2", target_bir_lowering=False, num_devices=1)
    args = {}
    for name, a in arrays.items():
        arrays[name] = a = _np.ascontiguousarray(a)
        args[name] = nc.dram_tensor(name, a.shape, _mybir.dt.from_np(a.dtype), kind="ExternalInput").ap()
    out = nc.dram_tensor("out", (OUT_ROWS, D), _mybir.dt.float32, kind="ExternalOutput").ap()
    gnn_program(nc, *args.values(), out)
    got = _run(nc, [arrays], core_ids=[0]).results[0]["out"]
    return got[:N_NODES]
```
